# Optimizing a Trainium2 kernel written in Bass

```python
import numpy as np
import jax
import jax.numpy as jnp

def _softmax(x, axis=-1):
    return jax.nn.softmax(x, axis=axis)
def _gelu(x):
    return jax.nn.gelu(x, approximate=True)
def _silu(x):
    return jax.nn.silu(x)
def _sigmoid(x):
    return jax.nn.sigmoid(x)
def _layernorm(x, axis=-1, eps=1e-5):
    m = jnp.mean(x, axis=axis, keepdims=True)
    v = jnp.var(x, axis=axis, keepdims=True)
    return (x - m) / jnp.sqrt(v + eps)
def _scatter_add(tgt, idx, src, axis=0):
    return tgt.at[idx].add(src)
def _segment_sum(src, seg, n):
    return jax.ops.segment_sum(src, seg, n)

kernel_name = 'mk_adj_resnorm_d2_adj_256_c15996'

def setup_inputs(seed: int = 0):
    np.random.seed(seed)
    _w = jnp.asarray
    def _rec_inputs():
        import jax
        import jax.numpy as jnp
        _gk = jax.random.key(seed)
        x = 7.22e-05 + 1 * jax.random.normal(jax.random.fold_in(_gk, 1), (16, 1024, 256), jnp.float32)
        _a = jax.random.bernoulli(jax.random.fold_in(_gk, 2), 0.00390625, (16, 1024, 1024))
        _a = jnp.logical_or(_a, jnp.swapaxes(_a, -1, -2))
        _a = jnp.logical_or(_a, jnp.eye(1024, dtype=bool))
        adj = _a.astype(jnp.int32)
        return x, adj
    x, adj = _rec_inputs()
    def _L0_gnn_setup():
        import jax, jax.numpy as jnp
        import numpy as np
        B, S, D = (64, 512, 256)

        def _leaky(x):
            return jnp.where(x >= 0, x, 0.2 * x)
        key = jax.random.key(seed)
        k = jax.random.split(key, 6)
        stdv = 1.0 / np.sqrt(D)
        return {'hidden': jax.random.normal(k[0], (B, S, D), dtype=jnp.float32), 'adj': jax.random.randint(k[1], (B, S, S), 0, 5, dtype=jnp.int32), 'a0': jax.random.uniform(k[2], (D, 1), jnp.float32, -stdv, stdv), 'a1': jax.random.uniform(k[3], (D, 1), jnp.float32, -stdv, stdv), 'a2': jax.random.uniform(k[4], (D, 1), jnp.float32, -stdv, stdv), 'a3': jax.random.uniform(k[5], (D, 1), jnp.float32, -stdv, stdv), 'bias': jnp.zeros((D,), dtype=jnp.float32)}
    _L0_gnn_all = _L0_gnn_setup()
    _L0_gnn_in = {k: v for k, v in _L0_gnn_all.items() if k in ('a0', 'a1', 'a2', 'a3', 'bias', )}
    del _L0_gnn_all

    def _L1_gnn_setup():
        import jax, jax.numpy as jnp
        import numpy as np
        ALPHA = 0.2
        key = jax.random.key(seed)
        k1, k2, k3, k4 = jax.random.split(key, 4)
        B, N, F_IN, F_OUT = (4, 4096, 256, 256)
        h = jax.random.normal(k1, (B, N, F_IN), dtype=jnp.float32)
        adj = jax.random.randint(k2, (B, N, N), 0, 2, dtype=jnp.int32)
        std_W = 1.414 * np.sqrt(2.0 / (F_IN + F_OUT))
        W = jax.random.normal(k3, (F_IN, F_OUT), dtype=jnp.float32) * std_W
        std_a = 1.414 * np.sqrt(2.0 / (1 + 2 * F_OUT))
        a = jax.random.normal(k4, (1, 2 * F_OUT), dtype=jnp.float32) * std_a
        return {'h': h, 'adj': adj, 'W': W, 'a': a}
    _L1_gnn_all = _L1_gnn_setup()
    _L1_gnn_in = {k: v for k, v in _L1_gnn_all.items() if k in ('W', 'a', )}
    del _L1_gnn_all

    return {
        "x": x,
        "adj": adj,
        "L0_gnn_a0": _L0_gnn_in["a0"],
        "L0_gnn_a1": _L0_gnn_in["a1"],
        "L0_gnn_a2": _L0_gnn_in["a2"],
        "L0_gnn_a3": _L0_gnn_in["a3"],
        "L0_gnn_bias": _L0_gnn_in["bias"],
        "L1_gnn_W": _L1_gnn_in["W"],
        "L1_gnn_a": _L1_gnn_in["a"],
    }

def reference(x, adj, L0_gnn_a0, L0_gnn_a1, L0_gnn_a2, L0_gnn_a3, L0_gnn_bias, L1_gnn_W, L1_gnn_a):
    import jax
    import jax.numpy as jnp
    def _L0_gnn_ref(hidden, adj, a0, a1, a2, a3, bias):
        import jax, jax.numpy as jnp
        import numpy as np
        B, S, D = (64, 512, 256)

        def _leaky(x):
            return jnp.where(x >= 0, x, 0.2 * x)
        h = hidden

        def e_of(a):
            return _leaky(jnp.einsum('bid,bjd->bij', h * a[:, 0], h))
        e0, e1, e2, e3 = (e_of(a0), e_of(a1), e_of(a2), e_of(a3))
        neg_inf = jnp.float32(-jnp.finfo(e0.dtype).max)
        alpha = jnp.where(adj == 1, e0, neg_inf)
        alpha = jnp.where(adj == 2, e1, alpha)
        alpha = jnp.where(adj == 3, e2, alpha)
        alpha = jnp.where(adj == 4, e3, alpha)
        alpha = jax.nn.sigmoid(alpha)
        return jnp.einsum('bij,bjd->bid', alpha, h) + bias

    def _L1_gnn_ref(h, adj, W, a):
        import jax, jax.numpy as jnp
        import numpy as np
        ALPHA = 0.2
        F_out = W.shape[1]
        Hh = jnp.einsum('bni,io->bno', h, W)
        a_src = a[0, :F_out]
        a_dst = a[0, F_out:]
        s = jnp.einsum('bno,o->bn', Hh, a_src)
        d = jnp.einsum('bno,o->bn', Hh, a_dst)
        logits = s[:, :, None] + d[:, None, :]
        e = jnp.where(adj != 0, jnp.exp(-jax.nn.leaky_relu(logits, negative_slope=ALPHA)), jnp.zeros((), dtype=Hh.dtype))
        rowsum = jnp.sum(e, axis=-1, keepdims=True)
        rowsum = jnp.where(rowsum == 0.0, 1.0, rowsum)
        h_prime = jnp.einsum('bnm,bmo->bno', e, Hh) / rowsum
        return jax.nn.elu(h_prime)

    x = _layernorm(x + _L0_gnn_ref(x, adj, L0_gnn_a0, L0_gnn_a1, L0_gnn_a2, L0_gnn_a3, L0_gnn_bias), axis=-1)
    x = _layernorm(x + _L1_gnn_ref(x, adj, L1_gnn_W, L1_gnn_a), axis=-1)
    return x


_drawn_inputs = setup_inputs


def setup_inputs(seed=0):
    import zlib

    import numpy as np

    out = dict(_drawn_inputs(seed))
    spreads = {'L0_gnn_bias': (0.0, 0.1)}
    factors = {}
    for name, (base, spread) in spreads.items():
        noise = np.random.default_rng([zlib.crc32(name.encode()), seed]).standard_normal(out[name].shape)
        drawn = base * np.exp(spread * noise) if base else spread * noise
        out[name] = jnp.asarray(drawn.astype(out[name].dtype))
    for name, factor in factors.items():
        out[name] = (out[name] * factor).astype(out[name].dtype)
    return out
```

```python
import numpy as np
import concourse.bass as bass
from concourse import mybir
from contextlib import ExitStack

P = 128
FP32 = mybir.dt.float32
FP32R = mybir.dt.float32r
BF16 = mybir.dt.bfloat16
INT32 = mybir.dt.int32
ALU = mybir.AluOpType
ACT = mybir.ActivationFunctionType
AX = mybir.AxisListType

SLOPE = 0.2
EPS = 1e-5
RANGE_MAX = 40.0
NOT_BINARY_BITS = -0x3F803F81


class Signals:

    def __init__(self, sem, tag):
        self.x_loaded = sem(tag + "x_loaded")
        self.adj_loaded = [sem(tag + f"adj_loaded{i}") for i in range(2)]
        self.out_stored = [sem(tag + f"out_stored{i}") for i in range(2)]
        self.xT = sem(tag + "xT")
        self.xT_hi = sem(tag + "xT_hi")
        self.xT_lo = sem(tag + "xT_lo")
        self.h_hi = sem(tag + "h_hi")
        self.h_lo = sem(tag + "h_lo")
        self.xb = sem(tag + "xb")
        self.logits = sem(tag + "logits")
        self.scaled = sem(tag + "scaled")
        self.leaky = sem(tag + "leaky")
        self.tanh = sem(tag + "tanh")
        self.plus1 = sem(tag + "plus1")
        self.gx = sem(tag + "gx")
        self.g_hi = sem(tag + "g_hi")
        self.g_lo = sem(tag + "g_lo")
        self.picked = sem(tag + "picked")
        self.summed = sem(tag + "summed")
        self.codes = sem(tag + "codes")
        self.codes_kept = sem(tag + "codes_kept")
        self.codes_seen = sem(tag + "codes_seen")
        self.mirror = sem(tag + "mirror")
        self.mirror_used = sem(tag + "mirror_used")
        self.mask0 = sem(tag + "mask0")
        self.hi0 = sem(tag + "hi0")
        self.lo0 = sem(tag + "lo0")
        self.agg0 = sem(tag + "agg0")
        self.resid0 = sem(tag + "resid0")
        self.stats0 = sem(tag + "stats0")
        self.moments0 = sem(tag + "moments0")
        self.var0 = sem(tag + "var0")
        self.rstd0 = sem(tag + "rstd0")
        self.x1 = sem(tag + "x1")
        self.x1T = sem(tag + "x1T")
        self.x1T_hi = sem(tag + "x1T_hi")
        self.x1T_lo = sem(tag + "x1T_lo")
        self.proj = sem(tag + "proj")
        self.sd = sem(tag + "sd")
        self.scale = sem(tag + "scale")
        self.H_hi = sem(tag + "H_hi")
        self.H_lo = sem(tag + "H_lo")
        self.ones_hi = sem(tag + "ones_hi")
        self.ones_lo = sem(tag + "ones_lo")
        self.squares = sem(tag + "squares")
        self.range_seen = sem(tag + "range_seen")
        self.sT = sem(tag + "sT")
        self.G = sem(tag + "G")
        self.pair = sem(tag + "pair")
        self.leaky1 = sem(tag + "leaky1")
        self.exp1 = sem(tag + "exp1")
        self.mask1 = sem(tag + "mask1")
        self.hi1 = sem(tag + "hi1")
        self.lo1 = sem(tag + "lo1")
        self.agg1 = sem(tag + "agg1")
        self.rowsum = sem(tag + "rowsum")
        self.rinv = sem(tag + "rinv")
        self.elu_exp = sem(tag + "elu_exp")
        self.relu = sem(tag + "relu")
        self.elu = sem(tag + "elu")
        self.resid1 = sem(tag + "resid1")
        self.stats1 = sem(tag + "stats1")
        self.moments1 = sem(tag + "moments1")
        self.var1 = sem(tag + "var1")
        self.rstd1 = sem(tag + "rstd1")
        self.y = sem(tag + "y")


def two_graph_layers(nc, x, adj, a0, a1, a2, a3, bias, W, a, out):
    B, N, D = x.shape
    NT = N // P
    KD = D // P
    HC = D + 2
    KINDS = 4

    ROWS = [0, 7, 6, 5, 1, 2, 3, 4]
    CHUNKS = []
    for J in ROWS:
        n = NT - J
        cut = J + (n + 1) // 2 if n > 4 else NT
        CHUNKS.append((J, J, cut))
        if cut < NT:
            CHUNKS.append((J, cut, NT))
    NCH = len(CHUNKS)
    ROW_END = {J: max(k for k in range(NCH) if CHUNKS[k][0] == J) + 1 for J in ROWS}
    MIRRORS = []
    for t in range(NT):
        for j in range(t + 1, NT, 4):
            MIRRORS.append((t, j, min(j + 4, NT)))
    NM = len(MIRRORS)

    x_v = x.rearrange("b (t p) d -> b p t d", p=P)
    adj_v = adj.rearrange("b (t p) j -> b t p j", p=P)
    out_v = out.rearrange("b (t p) d -> b t p d", p=P)

    ctx = ExitStack()
    with ctx:
        def sb(name, shape, dt=FP32):
            return ctx.enter_context(nc.sbuf_tensor(name, shape, dt))

        def bank(name):
            return ctx.enter_context(nc.psum_tensor(name, [P, 512], FP32))

        def sem(name):
            return ctx.enter_context(nc.semaphore(name))

        ident = sb("ident", [P, P])
        ident_bf = sb("ident_bf", [P, P], BF16)
        ones_col = sb("ones_col", [P, 1])
        neg_half = sb("neg_half", [P, 1])
        eps_col = sb("eps_col", [P, 1])
        a_col = sb("a_col", [P, KINDS, KD])
        bias_bc = sb("bias_bc", [P, D])
        a_bc = sb("a_bc", [P, 2 * D])
        W_ext = sb("W_ext", [P, KD, HC])
        W_hi = sb("W_hi", [P, KD, HC], FP32R)
        W_lo = sb("W_lo", [P, KD, HC], FP32R)
        x_raw = sb("x_raw", [P, NT, D])
        xb = sb("xb", [P, NT, D])
        h_hi = sb("h_hi", [P, NT, D], FP32R)
        h_lo = sb("h_lo", [P, NT, D], FP32R)
        hT_hi = sb("hT_hi", [P, KD, N], FP32R)
        hT_lo = sb("hT_lo", [P, KD, N], FP32R)
        gT_hi = sb("gT_hi", [P, KD, N], FP32R)
        gT_lo = sb("gT_lo", [P, KD, N], FP32R)
        gx = sb("gx", [P, KD, P])
        scaled = sb("scaled", [P, 2, 512])
        score = sb("score", [P, NT // 2, N + N // 2])
        code_nat = sb("code_nat", [P, 2, N], BF16)
        codeT = sb("codeT", [P, NT, N], BF16)
        watch_bits = sb("watch_bits", [P, N // 2], INT32)
        coef = sb("coef", [P, 2, N])
        coef_hi = sb("coef_hi", [P, 4, NT, P], FP32R)
        coef_lo = sb("coef_lo", [P, 4, NT, P], FP32R)
        resid = sb("resid", [P, 2, D])
        stats = sb("stats", [P, 2, 6])
        moments = sb("moments", [P, 2, 2])
        var_eps = sb("var_eps", [P, 2, 1])
        rstd = sb("rstd", [P, 2, 1])
        x1 = sb("x1", [P, NT, D])
        x1T_hi = sb("x1T_hi", [P, 2, KD, P], FP32R)
        x1T_lo = sb("x1T_lo", [P, 2, KD, P], FP32R)
        H_hi = sb("H_hi", [P, NT, HC], FP32R)
        H_lo = sb("H_lo", [P, NT, HC], FP32R)
        sd = sb("sd", [P, NT, 2])
        sd_sq = sb("sd_sq", [P, NT, 2])
        watch_range = sb("watch_range", [P, NT, 2])
        scale_col = sb("scale_col", [P, NT])
        E_col = sb("E_col", [P, NT])
        G = sb("G", [P, N])
        rowsum = sb("rowsum", [P, 2, 1])
        rinv = sb("rinv", [P, 2, 1])
        eluE = sb("eluE", [P, 2, D])
        reluP = sb("reluP", [P, 2, D])
        y_out = sb("y_out", [P, 2, D])
        flag_parts = sb("flag_parts", [P, 3])
        flag_f = sb("flag_f", [P, 1])
        flag_i = sb("flag_i", [1, 1], INT32)

        lg_bank = [bank(f"lg_bank{i}") for i in range(2)]
        acc_bank = [bank(f"acc_bank{i}") for i in range(2)]
        tr_bank = [bank(f"tr_bank{i}") for i in range(2)]
        xt_bank = bank("xt_bank")
        hh_bank = bank("hh_bank")

        F = Signals(sem, "f_")
        GEN = Signals(sem, "g_")
        weights_loaded = sem("weights_loaded")
        ident_made = sem("ident_made")
        consts_made = sem("consts_made")
        setup_step = sem("setup_step")
        weights_ready = sem("weights_ready")
        dve_past = sem("dve_past")
        sp_past = sem("sp_past")
        flag_step = sem("flag_step")
        flag_summed = sem("flag_summed")
        flag_ready = sem("flag_ready")

        N_WEIGHT_DMAS = KINDS + 3
        LAST = B - 1

        def f32(ap):
            return ap.bitcast(FP32)

        def score_at(J, c0, c1):
            if J < NT // 2:
                return score[:, J, c0 * P:c1 * P]
            return score[:, J - NT // 2, (c0 + NT // 2) * P:(c1 + NT // 2) * P]

        def blocks(ap):
            return ap.rearrange("p (j i) -> p j i", i=P)

        block = ctx.enter_context(nc.Block())

        @block.sync
        def _(sp):
            for k, ak in enumerate((a0, a1, a2, a3)):
                with nc.allow_non_contiguous_dma(reason="one column of 256 values"):
                    sp.dma_start(a_col[:, k, :], ak.rearrange("(c p) o -> p (c o)", p=P)).then_inc(weights_loaded, 16)
            sp.dma_start(W_ext[:, :, 0:D], W.rearrange("(c p) o -> p c o", p=P)).then_inc(weights_loaded, 16)
            sp.dma_start(bias_bc[:, :], bias.partition_broadcast(P)).then_inc(weights_loaded, 16)
            sp.dma_start(a_bc[:, :], a[0, :].partition_broadcast(P)).then_inc(weights_loaded, 16)

            def load_x(S, b):
                sp.dma_start(x_raw[:, :, :], x_v[b, :, :, :]).then_inc(S.x_loaded, 16)

            def store(S, b, t):
                sp.wait_ge(S.y, NT * b + t + 1)
                sp.sem_inc(sp_past, 1)
                sp.dma_start(out_v[b, t, :, :], y_out[:, t % 2, :]).then_inc(S.out_stored[t % 2], 16)

            def graph(b, nxt):
                if nxt:
                    sp.wait_ge(F.h_lo, 4 * b + 4)
                    sp.wait_ge(F.xb, NT * b + NT)
                    sp.wait_ge(F.xT, 4 * b + 4)
                    sp.sem_inc(sp_past, 1)
                    load_x(F, b + 1)
                for t in range(NT):
                    store(F, b, t)

            load_x(F, 0)
            with sp.Fori(0, LAST) as b:
                graph(b, True)
            graph(LAST, False)
            for s in F.out_stored:
                sp.wait_ge(s, 16 * B * NT // 2)

            sp.wait_ge(flag_ready, 1)
            flag = sp.value_load(flag_i[0:1, 0:1], min_val=0, max_val=512)
            with sp.If(flag > 0):
                with sp.Fori(0, B) as b:
                    load_x(GEN, b)
                    for t in range(NT):
                        store(GEN, b, t)
                    for s in GEN.out_stored:
                        sp.wait_ge(s, 64 * b + 64)
                    sp.sem_inc(sp_past, 1)

        @block.gpsimd
        def _(pool):
            nc.gpsimd.memset(ident[:, :], 0.0).then_inc(ident_made, 1)
            nc.gpsimd.memset(ident_bf[:, :], 0.0).then_inc(ident_made, 1)
            nc.gpsimd.memset(ones_col[:, :], 1.0).then_inc(consts_made, 1)
            nc.gpsimd.memset(neg_half[:, :], -0.5).then_inc(consts_made, 1)
            nc.gpsimd.memset(eps_col[:, :], EPS).then_inc(consts_made, 1)
            pool.wait_ge(ident_made, 2)
            for m in (ident, ident_bf):
                nc.gpsimd.affine_select(out=m[:, :], in_=m[:, :], compare_op=ALU.not_equal, fill=1.0, base=0,
                                        pattern=[[-1, P]], channel_multiplier=1).then_inc(ident_made, 1)

            def load_adj(S, b, t, first):
                if not first:
                    pool.wait_ge(S.codes, NT * b + t - 1)
                    if S is F:
                        pool.wait_ge(S.codes_seen, NT * b + t - 1)
                pool.dma_start(code_nat[:, t % 2, :], adj_v[b, t, :, :]).then_inc(S.adj_loaded[t % 2], 16)

            def low_x(S, b, c):
                pool.wait_ge(S.h_hi, 4 * b + c + 1)
                nc.gpsimd.tensor_tensor(h_lo[:, 2 * c:2 * c + 2, :], x_raw[:, 2 * c:2 * c + 2, :],
                                        f32(h_hi[:, 2 * c:2 * c + 2, :]), ALU.subtract).then_inc(S.h_lo, 1)

            def add_bias(S, b, t):
                nc.gpsimd.tensor_tensor(xb[:, t, :], x_raw[:, t, :], bias_bc[:, :], ALU.add).then_inc(S.xb, 1)

            def low0(S, b, t):
                pool.wait_ge(S.hi0, NT * b + t + 1)
                nc.gpsimd.tensor_tensor(coef_lo[:, t % 4, :, :], blocks(coef[:, t % 2, :]),
                                        f32(coef_hi[:, t % 4, :, :]), ALU.subtract).then_inc(S.lo0, 1)

            def low1(S, b, t):
                pool.wait_ge(S.hi1, NT * b + t + 1)
                nc.gpsimd.tensor_tensor(coef_lo[:, t % 4, :, :], blocks(coef[:, t % 2, :]),
                                        f32(coef_hi[:, t % 4, :, :]), ALU.subtract).then_inc(S.lo1, 1)

            def power(S, b, t, moments_made, var_made, rstd_made):
                pool.wait_ge(moments_made, NT * b + t + 1)
                nc.gpsimd.tensor_tensor(var_eps[:, t % 2, :], moments[:, t % 2, 1:2], eps_col[:, :],
                                        ALU.add).then_inc(var_made, 1)
                pool.wait_ge(var_made, NT * b + t + 1)
                nc.gpsimd.tensor_tensor(rstd[:, t % 2, :], var_eps[:, t % 2, :], neg_half[:, :],
                                        ALU.pow).then_inc(rstd_made, 1)

            def pair(b, t):
                if t == 0:
                    pool.wait_ge(GEN.ones_hi, b + 1)
                    pool.wait_ge(GEN.G, 2 * b + 2)
                s_b = G[:, t * P:(t + 1) * P].unsqueeze(1).broadcast_to([P, NT, P])
                d_b = E_col[:, :].unsqueeze(2).broadcast_to([P, NT, P])
                nc.gpsimd.tensor_tensor(blocks(coef[:, t % 2, :]), s_b, d_b, ALU.add).then_inc(GEN.pair, 1)

            def graph(b, nxt):
                low0(F, b, 0)
                low0(F, b, 1)
                for t in range(NT):
                    if t + 2 < NT:
                        low0(F, b, t + 2)
                    power(F, b, t, F.moments0, F.var0, F.rstd0)
                    if nxt and t >= 4:
                        for u in (2 * (t - 4), 2 * (t - 4) + 1):
                            if u == 0:
                                pool.wait_ge(F.x_loaded, 16 * (b + 2))
                            pool.wait_ge(F.resid0, NT * b + u + 1)
                            add_bias(F, b + 1, u)
                if nxt:
                    for t in range(2):
                        load_adj(F, b + 1, t, False)
                low1(F, b, 0)
                for t in range(NT):
                    if t + 1 < NT:
                        low1(F, b, t + 1)
                    if nxt:
                        if t + 2 < NT:
                            load_adj(F, b + 1, t + 2, False)
                        if 1 <= t <= 4:
                            low_x(F, b + 1, t - 1)
                    if t >= 1:
                        power(F, b, t - 1, F.moments1, F.var1, F.rstd1)
                power(F, b, NT - 1, F.moments1, F.var1, F.rstd1)

            pool.wait_ge(consts_made, 3)
            pool.wait_ge(F.x_loaded, 16)
            pool.wait_ge(weights_loaded, 16 * N_WEIGHT_DMAS)
            load_adj(F, 0, 0, True)
            load_adj(F, 0, 1, True)
            for t in range(NT):
                add_bias(F, 0, t)
            for c in range(4):
                low_x(F, 0, c)
            for t in range(2, NT):
                load_adj(F, 0, t, False)
            with pool.Fori(0, LAST) as b:
                graph(b, True)
            graph(LAST, False)

            pool.wait_ge(flag_ready, 1)
            flag = pool.value_load(flag_i[0:1, 0:1], min_val=0, max_val=512)
            with pool.If(flag > 0):
                with pool.Fori(0, B) as b:
                    pool.wait_ge(GEN.x_loaded, 16 * b + 16)
                    for t in range(NT):
                        add_bias(GEN, b, t)
                    for c in range(4):
                        low_x(GEN, b, c)
                    for t in range(NT):
                        load_adj(GEN, b, t, t < 2)
                        low0(GEN, b, t)
                        power(GEN, b, t, GEN.moments0, GEN.var0, GEN.rstd0)
                    for t in range(NT):
                        pair(b, t)
                        low1(GEN, b, t)
                        power(GEN, b, t, GEN.moments1, GEN.var1, GEN.rstd1)
                    for s in GEN.out_stored:
                        pool.wait_ge(s, 64 * b + 64)

        @block.scalar
        def _(act):
            def high_xT(S, b, c, general):
                act.wait_ge(S.xT, 4 * b + c + 1)
                if not general:
                    if not isinstance(b, int) or b > 0:
                        act.wait_ge(S.logits, NCH * b)
                cols = slice(2 * c * P, (2 * c + 2) * P)
                xt = xt_bank[:, :].rearrange("p (c i) -> p c i", c=KD)
                ins = nc.scalar.activation(hT_hi[:, :, cols], xt, ACT.Copy)
                if not general:
                    for dt in range(KD):
                        ins = nc.scalar.activation(gT_hi[:, dt, cols], xt[:, dt, :], ACT.Copy,
                                                   scale=a_col[:, 0, dt:dt + 1])
                ins.then_inc(S.xT_hi, 1)

            def high_x(S, b, c):
                if c == 0:
                    act.wait_ge(S.x_loaded, 16 * b + 16)
                    if S is F and (not isinstance(b, int) or b > 0):
                        act.wait_ge(S.agg0, NT * b)
                nc.scalar.activation(h_hi[:, 2 * c:2 * c + 2, :], x_raw[:, 2 * c:2 * c + 2, :],
                                     ACT.Copy).then_inc(S.h_hi, 1)

            def scale_scores(b, k):
                J, c0, c1 = CHUNKS[k]
                act.wait_ge(F.logits, NCH * b + k + 1)
                if not (isinstance(b, int) and b == 0 and k < 2):
                    act.wait_ge(F.leaky, NCH * b + k - 1)
                w = (c1 - c0) * P
                nc.scalar.activation(scaled[:, k % 2, 0:w], lg_bank[k % 2][:, 0:w], ACT.Copy,
                                     scale=SLOPE).then_inc(F.scaled, 1)

            def scale_row(b, J):
                for k in range(NCH):
                    if CHUNKS[k][0] == J:
                        scale_scores(b, k)

            def tanh_row(b, n):
                J = n
                act.wait_ge(F.leaky, NCH * b + NCH)
                nc.scalar.activation(score_at(J, J, NT), score_at(J, J, NT), ACT.Tanh,
                                     scale=0.5).then_inc(F.tanh, 1)

            def keep_codes(S, b, t, prev):
                act.wait_ge(S.codes, NT * b + t + 1)
                if prev:
                    act.wait_ge(S.mask1, NT * b + t + 1 - NT)
                nc.scalar.activation(codeT[:, t, :], tr_bank[t % 2][:, :].bitcast(BF16),
                                     ACT.Copy).then_inc(S.codes_kept, 1)

            def high0(S, b, t, prev):
                act.wait_ge(S.mask0, NT * b + t + 1)
                if t >= 4:
                    act.wait_ge(S.agg0, NT * b + t - 3)
                elif prev:
                    act.wait_ge(S.agg1, NT * b + t - 3)
                nc.scalar.activation(coef_hi[:, t % 4, :, :], blocks(coef[:, t % 2, :]),
                                     ACT.Copy).then_inc(S.hi0, 1)

            def high1(S, b, t):
                act.wait_ge(S.mask1, NT * b + t + 1)
                if t >= 4:
                    act.wait_ge(S.agg1, NT * b + t - 3)
                else:
                    act.wait_ge(S.agg0, NT * b + t + 5)
                nc.scalar.activation(coef_hi[:, t % 4, :, :], blocks(coef[:, t % 2, :]),
                                     ACT.Copy).then_inc(S.hi1, 1)

            def high_x1T(S, b, t, prev):
                act.wait_ge(S.x1T, NT * b + t + 1)
                if t >= 2 or prev:
                    act.wait_ge(S.proj, NT * b + t - 1)
                nc.scalar.activation(x1T_hi[:, t % 2, :, :],
                                     xt_bank[:, 0:D].rearrange("p (c i) -> p c i", c=KD),
                                     ACT.Copy).then_inc(S.x1T_hi, 1)

            def high_H(S, b, t, prev, general):
                act.wait_ge(S.proj, NT * b + t + 1)
                if prev and t == 0:
                    act.wait_ge(S.agg1, NT * b)
                nc.scalar.activation(scale_col[:, t:t + 1], hh_bank[:, D:D + 1], ACT.Exp,
                                     scale=0.0 if general else -SLOPE).then_inc(S.scale, 1)
                nc.scalar.activation(sd[:, t, :], hh_bank[:, D:D + 2], ACT.Copy).then_inc(S.sd, 1)
                act.wait_ge(S.scale, NT * b + t + 1)
                nc.scalar.activation(H_hi[:, t, 0:D], hh_bank[:, 0:D], ACT.Copy,
                                     scale=scale_col[:, t:t + 1]).then_inc(S.H_hi, 1)

            def ends_H(S, b, general):
                act.wait_ge(S.sd, NT * b + NT)
                if general:
                    nc.scalar.activation(E_col[:, :], sd[:, :, 0], ACT.Copy)
                else:
                    nc.scalar.activation(E_col[:, :], sd[:, :, 0], ACT.Exp, scale=SLOPE - 1.0)
                nc.scalar.activation(H_hi[:, :, D], scale_col[:, :], ACT.Copy).then_inc(S.ones_hi, 1)

            def make_G(S, b, c, general):
                act.wait_ge(S.sT, 2 * b + c + 1)
                dst = G[:, c * 512:(c + 1) * 512]
                if general:
                    nc.scalar.activation(dst, tr_bank[c][:, :], ACT.Copy).then_inc(S.G, 1)
                else:
                    nc.scalar.activation(dst, tr_bank[c][:, :], ACT.Exp, scale=1.0 - SLOPE).then_inc(S.G, 1)

            def elu_exp(S, b, t):
                act.wait_ge(S.rinv, NT * b + t + 1)
                if t >= 2 or not isinstance(b, int) or b > 0:
                    if S is F or t >= 2:
                        act.wait_ge(S.elu, NT * b + t - 1)
                nc.scalar.activation(eluE[:, t % 2, :], acc_bank[t % 2][:, 0:D], ACT.Exp,
                                     scale=rinv[:, t % 2, :]).then_inc(S.elu_exp, 1)

            def graph(b, prev, nxt):
                high0(F, b, 0, prev)
                high0(F, b, 1, prev)
                for t in range(NT):
                    if t + 2 < NT:
                        high0(F, b, t + 2, prev)
                    if t >= 2:
                        high_x1T(F, b, t - 2, prev)
                    if t >= 3:
                        high_H(F, b, t - 3, prev, False)
                    if nxt and 3 <= t < 7:
                        high_xT(F, b + 1, t - 3, False)
                if nxt:
                    scale_row(b + 1, 0)
                high_x1T(F, b, 6, prev)
                high_H(F, b, 5, prev, False)
                high_x1T(F, b, 7, prev)
                high_H(F, b, 6, prev, False)
                if nxt:
                    scale_row(b + 1, 7)
                    scale_row(b + 1, 6)
                high_H(F, b, 7, prev, False)
                ends_H(F, b, False)
                if nxt:
                    scale_row(b + 1, 5)
                make_G(F, b, 0, False)
                make_G(F, b, 1, False)
                if nxt:
                    scale_row(b + 1, 1)
                    scale_row(b + 1, 2)
                high1(F, b, 0)
                high1(F, b, 1)
                for t in range(NT):
                    if t + 2 < NT:
                        high1(F, b, t + 2)
                    if nxt:
                        keep_codes(F, b + 1, t, True)
                        if t < 2:
                            scale_row(b + 1, 3 + t)
                        if 1 <= t <= 4:
                            high_x(F, b + 1, t - 1)
                        if 3 <= t < 7:
                            tanh_row(b + 1, 2 * t - 6)
                            tanh_row(b + 1, 2 * t - 5)
                    elu_exp(F, b, t)

            act.wait_ge(weights_loaded, 16 * N_WEIGHT_DMAS)
            for c in range(4):
                high_xT(F, 0, c, False)
                high_x(F, 0, c)
            for J in ROWS:
                scale_row(0, J)
            for t in range(NT):
                keep_codes(F, 0, t, False)
            for J in range(NT):
                tanh_row(0, J)
            graph(0, False, True)
            with act.Fori(1, LAST) as b:
                graph(b, True, True)
            graph(LAST, True, False)

            act.wait_ge(flag_ready, 1)
            flag = act.value_load(flag_i[0:1, 0:1], min_val=0, max_val=512)
            with act.If(flag > 0):
                with act.Fori(0, B) as b:
                    for c in range(4):
                        high_xT(GEN, b, c, True)
                        high_x(GEN, b, c)
                    for t in range(NT):
                        keep_codes(GEN, b, t, False)
                        for k in range(KINDS):
                            n = KINDS * (NT * b + t) + k
                            act.wait_ge(GEN.logits, n + 1)
                            nc.scalar.activation(scaled[:, 0, :], lg_bank[0][:, :], ACT.Copy, scale=SLOPE)
                            nc.scalar.activation(scaled[:, 1, :], lg_bank[1][:, :], ACT.Copy,
                                                 scale=SLOPE).then_inc(GEN.scaled, 1)
                            act.wait_ge(GEN.leaky, n + 1)
                            nc.scalar.activation(score[:, 0, 0:N], score[:, 0, 0:N], ACT.Tanh,
                                                 scale=0.5).then_inc(GEN.tanh, 1)
                        high0(GEN, b, t, False)
                        high_x1T(GEN, b, t, False)
                        high_H(GEN, b, t, False, True)
                    ends_H(GEN, b, True)
                    make_G(GEN, b, 0, True)
                    make_G(GEN, b, 1, True)
                    for t in range(NT):
                        act.wait_ge(GEN.leaky1, NT * b + t + 1)
                        nc.scalar.activation(coef[:, t % 2, :], coef[:, t % 2, :], ACT.Exp,
                                             scale=-1.0).then_inc(GEN.exp1, 1)
                        high1(GEN, b, t)
                        elu_exp(GEN, b, t)
                    for s in GEN.out_stored:
                        act.wait_ge(s, 64 * b + 64)

        @block.vector
        def _(dve):
            nc.vector.memset(watch_bits[:, :], 0).then_inc(setup_step, 1)
            nc.vector.memset(watch_range[:, :, :], 0.0).then_inc(setup_step, 1)
            nc.vector.memset(sd_sq[:, :, :], 0.0).then_inc(setup_step, 1)
            dve.wait_ge(setup_step, 3)
            nc.vector.tensor_copy(H_hi[:, :, D + 1], sd_sq[:, :, 0]).then_inc(setup_step, 1)
            nc.vector.tensor_copy(H_lo[:, :, D + 1], sd_sq[:, :, 0]).then_inc(setup_step, 1)
            dve.wait_ge(weights_loaded, 16 * N_WEIGHT_DMAS)
            steps = 5
            for which, col in ((1, D), (0, D + 1)):
                for dt in range(KD):
                    nc.vector.tensor_tensor(reluP[:, 0, :], W_ext[:, dt, 0:D], a_bc[:, which * D:(which + 1) * D],
                                            ALU.mult).then_inc(setup_step, 1)
                    dve.wait_ge(setup_step, steps + 1)
                    nc.vector.tensor_reduce(W_ext[:, dt, col:col + 1], reluP[:, 0, :], AX.X,
                                            ALU.add).then_inc(setup_step, 1)
                    dve.wait_ge(setup_step, steps + 2)
                    steps += 2
            nc.vector.tensor_copy(W_hi[:, :, :], W_ext[:, :, :]).then_inc(setup_step, 1)
            dve.wait_ge(setup_step, steps + 1)
            nc.vector.tensor_tensor(W_lo[:, :, :], W_ext[:, :, :], f32(W_hi[:, :, :]),
                                    ALU.subtract).then_inc(weights_ready, 1)

            def low_xT(S, b, c, general):
                dve.wait_ge(S.xT_hi, 4 * b + c + 1)
                cols = slice(2 * c * P, (2 * c + 2) * P)
                xt = xt_bank[:, :].rearrange("p (c i) -> p c i", c=KD)
                ins = nc.vector.tensor_tensor(hT_lo[:, :, cols], xt, f32(hT_hi[:, :, cols]), ALU.subtract)
                if not general:
                    for dt in range(KD):
                        ins = nc.vector.scalar_tensor_tensor(gT_lo[:, dt, cols], xt[:, dt, :],
                                                             a_col[:, 0, dt:dt + 1], f32(gT_hi[:, dt, cols]),
                                                             ALU.mult, ALU.subtract)
                ins.then_inc(S.xT_lo, 1)

            def leaky_scores(b, k):
                J, c0, c1 = CHUNKS[k]
                if k == 0 and not (isinstance(b, int) and b == 0):
                    dve.wait_ge(F.mask0, NT * b)
                dve.wait_ge(F.scaled, NCH * b + k + 1)
                w = (c1 - c0) * P
                nc.vector.tensor_tensor(score_at(J, c0, c1), lg_bank[k % 2][:, 0:w], scaled[:, k % 2, 0:w],
                                        ALU.max).then_inc(F.leaky, 1)

            def leaky_row(b, J):
                for k in range(NCH):
                    if CHUNKS[k][0] == J:
                        leaky_scores(b, k)

            def see_codes(S, b, t):
                slot = t % 2
                dve.wait_ge(S.adj_loaded[slot], 64 * b + 16 * (t // 2) + 16)
                if not (isinstance(b, int) and b == 0 and t == 0):
                    dve.wait_ge(S.codes_seen, NT * b + t)
                nc.vector.tensor_tensor(watch_bits[:, :], watch_bits[:, :], code_nat[:, slot, :].bitcast(INT32),
                                        ALU.bitwise_or).then_inc(S.codes_seen, 1)

            def mask0(b, t, prev):
                if t == 0:
                    dve.wait_ge(F.tanh, NT * b + NT)
                    dve.wait_ge(F.codes_kept, NT * b + NT)
                if t >= 2:
                    dve.wait_ge(F.lo0, NT * b + t - 1)
                elif prev:
                    dve.wait_ge(F.lo1, NT * b + t - 1)
                for m, (tt, j0, j1) in enumerate(MIRRORS):
                    if tt == t:
                        dve.wait_ge(F.mirror, NM * b + m + 1)
                        nc.vector.scalar_tensor_tensor(
                            coef[:, t % 2, j0 * P:j1 * P], tr_bank[m % 2][:, 0:(j1 - j0) * P], 1.0,
                            codeT[:, t, j0 * P:j1 * P], ALU.add, ALU.mult).then_inc(F.mirror_used, 1)
                for j0, j1 in ((0, min(t + 1, NT // 2)), (NT // 2, t + 1)):
                    if j0 < j1:
                        at = t * P + j0 * P
                        ins = nc.vector.scalar_tensor_tensor(
                            blocks(coef[:, t % 2, j0 * P:j1 * P]), score[:, 0:j1 - j0, at:at + P], 1.0,
                            blocks(codeT[:, t, j0 * P:j1 * P]), ALU.add, ALU.mult)
                ins.then_inc(F.mask0, 1)

            def residual0(S, b, t, prev):
                if t >= 2:
                    dve.wait_ge(S.x1, NT * b + t - 1)
                elif prev:
                    dve.wait_ge(S.y, NT * b + t - 1)
                dve.wait_ge(S.agg0, NT * b + t + 1)
                if t == 0:
                    dve.wait_ge(S.xb, NT * b + NT)
                nc.vector.scalar_tensor_tensor(resid[:, t % 2, :], acc_bank[t % 2][:, 0:D], 0.5, xb[:, t, :],
                                               ALU.mult, ALU.add).then_inc(S.resid0, 1)
                dve.wait_ge(S.resid0, NT * b + t + 1)
                nc.vector.bn_stats(stats[:, t % 2, :], resid[:, t % 2, :]).then_inc(S.stats0, 1)
                dve.wait_ge(S.stats0, NT * b + t + 1)
                dve.sem_inc(dve_past, 1)
                nc.vector.bn_aggr(moments[:, t % 2, :], stats[:, t % 2, :]).then_inc(S.moments0, 1)

            def norm0(S, b, t):
                dve.wait_ge(S.rstd0, NT * b + t + 1)
                nc.vector.tensor_scalar(x1[:, t, :], resid[:, t % 2, :], moments[:, t % 2, 0:1],
                                        rstd[:, t % 2, :], ALU.subtract, ALU.mult).then_inc(S.x1, 1)

            def low_x1T(S, b, t):
                dve.wait_ge(S.x1T_hi, NT * b + t + 1)
                nc.vector.tensor_tensor(x1T_lo[:, t % 2, :, :],
                                        xt_bank[:, 0:D].rearrange("p (c i) -> p c i", c=KD),
                                        f32(x1T_hi[:, t % 2, :, :]), ALU.subtract).then_inc(S.x1T_lo, 1)

            def low_H(S, b, t):
                dve.wait_ge(S.H_hi, NT * b + t + 1)
                nc.vector.scalar_tensor_tensor(H_lo[:, t, 0:D], hh_bank[:, 0:D], scale_col[:, t:t + 1],
                                               f32(H_hi[:, t, 0:D]), ALU.mult, ALU.subtract).then_inc(S.H_lo, 1)

            def ends_H(S, b, prev):
                if prev:
                    dve.wait_ge(S.range_seen, b)
                dve.wait_ge(S.ones_hi, b + 1)
                nc.vector.tensor_tensor(H_lo[:, :, D], scale_col[:, :], f32(H_hi[:, :, D]),
                                        ALU.subtract).then_inc(S.ones_lo, 1)
                nc.vector.tensor_tensor(sd_sq[:, :, :], sd[:, :, :], sd[:, :, :], ALU.mult).then_inc(S.squares, 1)
                dve.wait_ge(S.squares, b + 1)
                nc.vector.tensor_tensor(watch_range[:, :, :], watch_range[:, :, :], sd_sq[:, :, :],
                                        ALU.max).then_inc(S.range_seen, 1)

            def mask1(b, t):
                if t == 0:
                    dve.wait_ge(F.ones_hi, b + 1)
                    dve.wait_ge(F.G, 2 * b + 2)
                if t < 2:
                    dve.wait_ge(F.lo0, NT * b + NT - 1 + t)
                else:
                    dve.wait_ge(F.lo1, NT * b + t - 1)
                for J in range(NT):
                    ins = nc.vector.scalar_tensor_tensor(
                        coef[:, t % 2, J * P:(J + 1) * P], G[:, t * P:(t + 1) * P], E_col[:, J:J + 1],
                        codeT[:, t, J * P:(J + 1) * P], ALU.min, ALU.mult)
                ins.then_inc(F.mask1, 1)

            def row_inverse(S, b, t, prev):
                if t >= 2 or prev:
                    dve.wait_ge(S.rinv, NT * b + t - 1)
                dve.wait_ge(S.agg1, NT * b + t + 1)
                nc.vector.tensor_scalar(rowsum[:, t % 2, :], acc_bank[t % 2][:, D:D + 1], 0.0, None,
                                        ALU.is_equal).then_inc(S.rowsum, 1)
                dve.wait_ge(S.rowsum, 2 * (NT * b + t) + 1)
                nc.vector.tensor_tensor(rowsum[:, t % 2, :], acc_bank[t % 2][:, D:D + 1], rowsum[:, t % 2, :],
                                        ALU.add).then_inc(S.rowsum, 1)
                dve.wait_ge(S.rowsum, 2 * (NT * b + t) + 2)
                nc.vector.reciprocal(rinv[:, t % 2, :], rowsum[:, t % 2, :]).then_inc(S.rinv, 1)

            def residual1(S, b, t):
                if t >= 2:
                    dve.wait_ge(S.y, NT * b + t - 1)
                else:
                    dve.wait_ge(S.x1, NT * b + t + 7)
                dve.wait_ge(S.elu_exp, NT * b + t + 1)
                nc.vector.tensor_scalar(reluP[:, t % 2, :], acc_bank[t % 2][:, 0:D], rinv[:, t % 2, :], 0.0,
                                        ALU.mult, ALU.max).then_inc(S.relu, 1)
                dve.wait_ge(S.relu, NT * b + t + 1)
                nc.vector.scalar_tensor_tensor(reluP[:, t % 2, :], eluE[:, t % 2, :], 1.0, reluP[:, t % 2, :],
                                               ALU.min, ALU.add).then_inc(S.elu, 1)
                dve.wait_ge(S.elu, NT * b + t + 1)
                nc.vector.scalar_tensor_tensor(resid[:, t % 2, :], reluP[:, t % 2, :], -1.0, x1[:, t, :],
                                               ALU.add, ALU.add).then_inc(S.resid1, 1)
                dve.wait_ge(S.resid1, NT * b + t + 1)
                nc.vector.bn_stats(stats[:, t % 2, :], resid[:, t % 2, :]).then_inc(S.stats1, 1)
                dve.wait_ge(S.stats1, NT * b + t + 1)
                dve.sem_inc(dve_past, 1)
                nc.vector.bn_aggr(moments[:, t % 2, :], stats[:, t % 2, :]).then_inc(S.moments1, 1)

            def norm1(S, b, t, prev):
                dve.wait_ge(S.rstd1, NT * b + t + 1)
                if prev or t >= 2:
                    dve.wait_ge(S.out_stored[t % 2], 64 * b + 16 * (t // 2))
                nc.vector.tensor_scalar(y_out[:, t % 2, :], resid[:, t % 2, :], moments[:, t % 2, 0:1],
                                        rstd[:, t % 2, :], ALU.subtract, ALU.mult).then_inc(S.y, 1)

            def graph(b, prev, nxt):
                mask0(b, 0, prev)
                mask0(b, 1, prev)
                for t in range(NT):
                    if t + 2 < NT:
                        mask0(b, t + 2, prev)
                    residual0(F, b, t, prev)
                    if t >= 1:
                        norm0(F, b, t - 1)
                    if t >= 2:
                        low_x1T(F, b, t - 2)
                    if t >= 3:
                        low_H(F, b, t - 3)
                    if nxt and 3 <= t < 7:
                        low_xT(F, b + 1, t - 3, False)
                if nxt:
                    leaky_row(b + 1, 0)
                norm0(F, b, 7)
                low_x1T(F, b, 6)
                low_H(F, b, 5)
                low_x1T(F, b, 7)
                low_H(F, b, 6)
                if nxt:
                    leaky_row(b + 1, 7)
                    leaky_row(b + 1, 6)
                low_H(F, b, 7)
                ends_H(F, b, prev)
                if nxt:
                    leaky_row(b + 1, 5)
                    leaky_row(b + 1, 1)
                    leaky_row(b + 1, 2)
                mask1(b, 0)
                mask1(b, 1)
                for t in range(NT):
                    if t + 2 < NT:
                        mask1(b, t + 2)
                    if nxt and t < 2:
                        leaky_row(b + 1, 3 + t)
                    row_inverse(F, b, t, prev)
                    if nxt:
                        see_codes(F, b + 1, t)
                    residual1(F, b, t)
                    if t >= 1:
                        norm1(F, b, t - 1, prev)
                norm1(F, b, NT - 1, prev)

            for c in range(4):
                low_xT(F, 0, c, False)
            for J in ROWS:
                leaky_row(0, J)
            for t in range(NT):
                see_codes(F, 0, t)
            graph(0, False, True)
            with dve.Fori(1, LAST) as b:
                graph(b, True, True)
            graph(LAST, True, False)

            dve.wait_ge(F.codes_seen, NT * B)
            dve.wait_ge(F.range_seen, B)
            nc.vector.tensor_scalar(watch_bits[:, :], watch_bits[:, :], NOT_BINARY_BITS, None,
                                    ALU.bitwise_and).then_inc(flag_step, 1)
            dve.wait_ge(flag_step, 1)
            nc.vector.tensor_scalar(coef[:, 0, 0:N // 2], watch_bits[:, :], 0.0, None,
                                    ALU.not_equal).then_inc(flag_step, 1)
            dve.wait_ge(flag_step, 2)
            nc.vector.tensor_reduce(flag_parts[:, 0:1], coef[:, 0, 0:N // 2], AX.X, ALU.max).then_inc(flag_step, 1)
            nc.vector.tensor_reduce(flag_parts[:, 1:2], watch_range[:, :, :], AX.XY, ALU.max).then_inc(flag_step, 1)
            dve.wait_ge(flag_step, 4)
            nc.vector.tensor_scalar(flag_parts[:, 2:3], flag_parts[:, 1:2], RANGE_MAX * RANGE_MAX, None,
                                    ALU.is_gt).then_inc(flag_step, 1)
            dve.wait_ge(flag_step, 5)
            nc.vector.tensor_tensor(flag_f[:, :], flag_parts[:, 0:1], flag_parts[:, 2:3],
                                    ALU.add).then_inc(flag_step, 1)
            dve.wait_ge(flag_summed, 1)
            nc.vector.tensor_copy(flag_i[:, :], xt_bank[0:1, 0:1]).then_inc(flag_ready, 1)

            dve.wait_ge(flag_ready, 1)
            flag = dve.value_load(flag_i[0:1, 0:1], min_val=0, max_val=512)
            with dve.If(flag > 0):
                with dve.Fori(0, B) as b:
                    for c in range(4):
                        low_xT(GEN, b, c, True)
                    for t in range(NT):
                        cols = slice(t * P, (t + 1) * P)
                        dve.wait_ge(GEN.xT_lo, 4 * b + 4)
                        if t:
                            dve.wait_ge(GEN.logits, KINDS * (NT * b + t))
                        nc.vector.tensor_tensor(gx[:, :, :], f32(hT_hi[:, :, cols]), f32(hT_lo[:, :, cols]),
                                                ALU.add).then_inc(GEN.gx, 1)
                        dve.wait_ge(GEN.gx, NT * b + t + 1)
                        for k in range(KINDS):
                            n = KINDS * (NT * b + t) + k
                            if k:
                                dve.wait_ge(GEN.logits, n)
                            for dt in range(KD):
                                ins = nc.vector.tensor_scalar(gT_hi[:, dt, 0:P], gx[:, dt, :],
                                                              a_col[:, k, dt:dt + 1], None, ALU.mult)
                            ins.then_inc(GEN.g_hi, 1)
                            dve.wait_ge(GEN.g_hi, n + 1)
                            for dt in range(KD):
                                ins = nc.vector.scalar_tensor_tensor(gT_lo[:, dt, 0:P], gx[:, dt, :],
                                                                     a_col[:, k, dt:dt + 1],
                                                                     f32(gT_hi[:, dt, 0:P]), ALU.mult, ALU.subtract)
                            ins.then_inc(GEN.g_lo, 1)
                            dve.wait_ge(GEN.scaled, n + 1)
                            nc.vector.tensor_tensor(score[:, 0, 0:512], lg_bank[0][:, :], scaled[:, 0, :], ALU.max)
                            nc.vector.tensor_tensor(score[:, 0, 512:N], lg_bank[1][:, :], scaled[:, 1, :],
                                                    ALU.max).then_inc(GEN.leaky, 1)
                            dve.wait_ge(GEN.tanh, n + 1)
                            nc.vector.tensor_scalar(score[:, 0, 0:N], score[:, 0, 0:N], 1.0, None,
                                                    ALU.add).then_inc(GEN.plus1, 1)
                            dve.wait_ge(GEN.plus1, n + 1)
                            if k == 0:
                                dve.wait_ge(GEN.codes_kept, NT * b + t + 1)
                                if t >= 2:
                                    dve.wait_ge(GEN.lo0, NT * b + t - 1)
                            dst = coef[:, t % 2, :] if k == 0 else score[:, 0, 0:N]
                            nc.vector.scalar_tensor_tensor(dst, codeT[:, t, :], float(k + 1), score[:, 0, 0:N],
                                                           ALU.is_equal, ALU.mult).then_inc(GEN.picked, 1)
                            dve.wait_ge(GEN.picked, n + 1)
                            if k:
                                ins = nc.vector.tensor_tensor(coef[:, t % 2, :], coef[:, t % 2, :],
                                                              score[:, 0, 0:N], ALU.add)
                                ins.then_inc(GEN.mask0 if k == KINDS - 1 else GEN.summed, 1)
                                if k < KINDS - 1:
                                    dve.wait_ge(GEN.summed, 2 * (NT * b + t) + k)
                        residual0(GEN, b, t, False)
                        norm0(GEN, b, t)
                        low_x1T(GEN, b, t)
                        low_H(GEN, b, t)
                    ends_H(GEN, b, False)
                    for t in range(NT):
                        dve.wait_ge(GEN.pair, NT * b + t + 1)
                        nc.vector.scalar_tensor_tensor(coef[:, t % 2, :], coef[:, t % 2, :], SLOPE,
                                                       coef[:, t % 2, :], ALU.mult, ALU.max).then_inc(GEN.leaky1, 1)
                        dve.wait_ge(GEN.exp1, NT * b + t + 1)
                        nc.vector.scalar_tensor_tensor(coef[:, t % 2, :], codeT[:, t, :], 0.0, coef[:, t % 2, :],
                                                       ALU.not_equal, ALU.mult).then_inc(GEN.mask1, 1)
                        row_inverse(GEN, b, t, False)
                        residual1(GEN, b, t)
                        norm1(GEN, b, t, False)
                    for s in GEN.out_stored:
                        dve.wait_ge(s, 64 * b + 64)

        @block.tensor
        def _(pe):
            def split_products(dst, lhs_hi, lhs_lo, rhs_hi, rhs_lo, first, last):
                nc.tensor.matmul(dst, lhs_hi, rhs_hi, start=first, stop=False)
                nc.tensor.matmul(dst, lhs_hi, rhs_lo, start=False, stop=False)
                return nc.tensor.matmul(dst, lhs_lo, rhs_hi, start=False, stop=last)

            def transpose_x(S, b, c):
                for i in range(2):
                    for dt in range(KD):
                        ins = nc.tensor.transpose(xt_bank[:, (2 * dt + i) * P:(2 * dt + i + 1) * P],
                                                  x_raw[:, 2 * c + i, dt * P:(dt + 1) * P], ident[:, :])
                ins.then_inc(S.xT, 1)

            def scores(b, J):
                for k in range(NCH):
                    if CHUNKS[k][0] != J:
                        continue
                    _, c0, c1 = CHUNKS[k]
                    if not (isinstance(b, int) and b == 0 and k < 2):
                        pe.wait_ge(F.leaky, NCH * b + k - 1)
                    dst = lg_bank[k % 2][:, 0:(c1 - c0) * P]
                    for dt in range(KD):
                        rows = slice(J * P, (J + 1) * P)
                        cols = slice(c0 * P, c1 * P)
                        ins = split_products(dst, gT_hi[:, dt, rows], gT_lo[:, dt, rows], hT_hi[:, dt, cols],
                                             hT_lo[:, dt, cols], dt == 0, dt == KD - 1)
                    ins.then_inc(F.logits, 1)

            def transpose_codes(S, b, t):
                pe.wait_ge(S.adj_loaded[t % 2], 64 * b + 16 * (t // 2) + 16)
                bank_bf = tr_bank[t % 2][:, :].bitcast(BF16)
                for J in range(NT):
                    ins = nc.tensor.transpose(bank_bf[:, J * P:(J + 1) * P],
                                              code_nat[:, t % 2, J * P:(J + 1) * P], ident_bf[:, :])
                ins.then_inc(S.codes, 1)

            def mirror(b, t):
                for m, (tt, j0, j1) in enumerate(MIRRORS):
                    if tt != t:
                        continue
                    if m >= 2:
                        pe.wait_ge(F.mirror_used, NM * b + m - 1)
                    else:
                        pe.wait_ge(F.codes_kept, NT * b + NT - 1 + m)
                        pe.wait_ge(F.tanh, NT * b + NT)
                    for j in range(j0, j1):
                        ins = nc.tensor.transpose(tr_bank[m % 2][:, (j - j0) * P:(j - j0 + 1) * P],
                                                  score_at(t, j, j + 1), ident[:, :])
                    ins.then_inc(F.mirror, 1)

            def aggregate0(S, b, t, prev):
                pe.wait_ge(S.lo0, NT * b + t + 1)
                if t == 0:
                    pe.wait_ge(S.h_lo, 4 * b + 4)
                if t >= 2:
                    pe.wait_ge(S.resid0, NT * b + t - 1)
                elif prev:
                    pe.wait_ge(S.relu, NT * b + t - 1)
                for J in range(NT):
                    ins = split_products(acc_bank[t % 2][:, 0:D], coef_hi[:, t % 4, J, :], coef_lo[:, t % 4, J, :],
                                         h_hi[:, J, :], h_lo[:, J, :], J == 0, J == NT - 1)
                ins.then_inc(S.agg0, 1)

            def transpose_x1(S, b, t):
                pe.wait_ge(S.x1, NT * b + t + 1)
                for dt in range(KD):
                    ins = nc.tensor.transpose(xt_bank[:, dt * P:(dt + 1) * P], x1[:, t, dt * P:(dt + 1) * P],
                                              ident[:, :])
                ins.then_inc(S.x1T, 1)

            def project(S, b, t, prev):
                pe.wait_ge(S.x1T_lo, NT * b + t + 1)
                if t >= 1 or prev:
                    pe.wait_ge(S.H_lo, NT * b + t)
                for dt in range(KD):
                    ins = split_products(hh_bank[:, 0:HC], x1T_hi[:, t % 2, dt, :], x1T_lo[:, t % 2, dt, :],
                                         W_hi[:, dt, :], W_lo[:, dt, :], dt == 0, dt == KD - 1)
                ins.then_inc(S.proj, 1)

            def spread_s(S, b, c):
                if c == 0:
                    pe.wait_ge(S.sd, NT * b + NT)
                for i in range(4):
                    t = 4 * c + i
                    ins = nc.tensor.transpose(tr_bank[c][:, i * P:(i + 1) * P],
                                              sd[:, t, 1:2].broadcast_to([P, P]), ident[:, :])
                ins.then_inc(S.sT, 1)

            def aggregate1(S, b, t):
                pe.wait_ge(S.lo1, NT * b + t + 1)
                if t == 0:
                    pe.wait_ge(S.ones_lo, b + 1)
                    pe.wait_ge(S.H_lo, NT * b + NT)
                if t >= 2:
                    pe.wait_ge(S.relu, NT * b + t - 1)
                else:
                    pe.wait_ge(S.resid0, NT * b + t + 7)
                for J in range(NT):
                    ins = split_products(acc_bank[t % 2][:, 0:HC], coef_hi[:, t % 4, J, :],
                                         coef_lo[:, t % 4, J, :], H_hi[:, J, :], H_lo[:, J, :],
                                         J == 0, J == NT - 1)
                ins.then_inc(S.agg1, 1)

            def graph(b, prev, nxt):
                mirror(b, 0)
                mirror(b, 1)
                for t in range(NT):
                    if t + 2 < NT:
                        mirror(b, t + 2)
                    aggregate0(F, b, t, prev)
                    if t >= 2:
                        if t == 2:
                            if prev:
                                pe.wait_ge(F.x1T_lo, NT * b)
                            else:
                                pe.wait_ge(F.xT_lo, 4)
                        elif t == 3 or not nxt:
                            pe.wait_ge(F.x1T_lo, NT * b + t - 2)
                        else:
                            pe.wait_ge(F.xT_lo, 4 * (b + 1) + t - 3)
                        transpose_x1(F, b, t - 2)
                    if t >= 3:
                        project(F, b, t - 3, prev)
                    if nxt and 3 <= t < 7:
                        if t == 3:
                            pe.wait_ge(F.x_loaded, 16 * (b + 2))
                        pe.wait_ge(F.x1T_lo, NT * b + t - 1)
                        transpose_x(F, b + 1, t - 3)
                if nxt:
                    pe.wait_ge(F.xT_lo, 4 * (b + 1) + 4)
                    scores(b + 1, 0)
                pe.wait_ge(F.x1T_lo, NT * b + 6)
                transpose_x1(F, b, 6)
                project(F, b, 5, prev)
                pe.wait_ge(F.x1T_lo, NT * b + 7)
                transpose_x1(F, b, 7)
                project(F, b, 6, prev)
                if nxt:
                    scores(b + 1, 7)
                    scores(b + 1, 6)
                project(F, b, 7, prev)
                if nxt:
                    scores(b + 1, 5)
                pe.wait_ge(F.mirror_used, NM * b + NM)
                spread_s(F, b, 0)
                spread_s(F, b, 1)
                if nxt:
                    scores(b + 1, 1)
                    scores(b + 1, 2)
                for t in range(NT):
                    aggregate1(F, b, t)
                    if nxt:
                        if t < 2:
                            pe.wait_ge(F.G, 2 * b + 1 + t)
                        else:
                            pe.wait_ge(F.codes_kept, NT * (b + 1) + t - 1)
                        transpose_codes(F, b + 1, t)
                        if t < 2:
                            scores(b + 1, 3 + t)

            pe.wait_ge(ident_made, 4)
            pe.wait_ge(F.x_loaded, 16)
            for c in range(4):
                if c:
                    pe.wait_ge(F.xT_lo, c)
                transpose_x(F, 0, c)
            pe.wait_ge(F.xT_lo, 4)
            for J in ROWS:
                scores(0, J)
            for t in range(NT):
                if t >= 2:
                    pe.wait_ge(F.codes_kept, t - 1)
                transpose_codes(F, 0, t)
            pe.wait_ge(weights_ready, 1)
            graph(0, False, True)
            with pe.Fori(1, LAST) as b:
                graph(b, True, True)
            graph(LAST, True, False)

            pe.wait_ge(flag_step, 6)
            pe.wait_ge(consts_made, 3)
            nc.tensor.matmul(xt_bank[0:1, 0:1], flag_f[:, :], ones_col[:, :], start=True,
                             stop=True).then_inc(flag_summed, 1)

            pe.wait_ge(flag_ready, 1)
            flag = pe.value_load(flag_i[0:1, 0:1], min_val=0, max_val=512)
            with pe.If(flag > 0):
                with pe.Fori(0, B) as b:
                    pe.wait_ge(GEN.x_loaded, 16 * b + 16)
                    for c in range(4):
                        if c:
                            pe.wait_ge(GEN.xT_lo, 4 * b + c)
                        transpose_x(GEN, b, c)
                    pe.wait_ge(GEN.xT_lo, 4 * b + 4)
                    for t in range(NT):
                        if t >= 2:
                            pe.wait_ge(GEN.codes_kept, NT * b + t - 1)
                        transpose_codes(GEN, b, t)
                        for k in range(KINDS):
                            n = KINDS * (NT * b + t) + k
                            pe.wait_ge(GEN.g_lo, n + 1)
                            for J in range(NT):
                                dst = lg_bank[J // 4][:, (J % 4) * P:(J % 4 + 1) * P]
                                rows = slice(J * P, (J + 1) * P)
                                for dt in range(KD):
                                    ins = split_products(dst, hT_hi[:, dt, rows], hT_lo[:, dt, rows],
                                                         gT_hi[:, dt, 0:P], gT_lo[:, dt, 0:P],
                                                         dt == 0, dt == KD - 1)
                            ins.then_inc(GEN.logits, 1)
                        aggregate0(GEN, b, t, False)
                        if t:
                            pe.wait_ge(GEN.x1T_lo, NT * b + t)
                        transpose_x1(GEN, b, t)
                        project(GEN, b, t, False)
                    pe.wait_ge(GEN.codes_kept, NT * b + NT)
                    spread_s(GEN, b, 0)
                    spread_s(GEN, b, 1)
                    for t in range(NT):
                        aggregate1(GEN, b, t)
                    for s in GEN.out_stored:
                        pe.wait_ge(s, 64 * b + 64)


_INS = ["x", "adj", "L0_gnn_a0", "L0_gnn_a1", "L0_gnn_a2", "L0_gnn_a3", "L0_gnn_bias", "L1_gnn_W", "L1_gnn_a"]


def kernel(**inputs):
    import concourse.bacc as bacc
    from concourse.bass_utils import run_bass_kernel_spmd

    nc = bacc.Bacc("TRN2", target_bir_lowering=False, num_devices=1)
    arrays, args = {}, []
    for name in _INS:
        v = np.ascontiguousarray(inputs[name])
        arrays["in_" + name] = v
        args.append(nc.dram_tensor("in_" + name, v.shape, mybir.dt.from_np(v.dtype), kind="ExternalInput").ap())
    shape = inputs["x"].shape
    out = nc.dram_tensor("out_0", shape, FP32, kind="ExternalOutput").ap()
    two_graph_layers(nc, *args, out)
    r = run_bass_kernel_spmd(nc, [arrays], core_ids=[0])
    return r.results[0]["out_0"]
```

```python
import numpy as np
import concourse.bass as bass
from concourse import mybir
from contextlib import ExitStack

P = 128
FP32 = mybir.dt.float32
FP32R = mybir.dt.float32r
BF16 = mybir.dt.bfloat16
INT32 = mybir.dt.int32
ALU = mybir.AluOpType
ACT = mybir.ActivationFunctionType
AX = mybir.AxisListType

SLOPE = 0.2
EPS = 1e-5
RANGE_MAX = 40.0
LEAST_ROWSUM = 1e-30


class Signals:

    def __init__(self, sem, tag, general):
        self.x_loaded = sem(tag + "x_loaded")
        self.adj_loaded = [sem(tag + f"adj_loaded{i}") for i in range(4)]
        self.out_stored = [sem(tag + f"out_stored{i}") for i in range(1 if general else 8)]
        self.xT = sem(tag + "xT")
        self.xT_hi = sem(tag + "xT_hi")
        self.xT_lo = sem(tag + "xT_lo")
        self.h_hi = sem(tag + "h_hi")
        self.h_lo = sem(tag + "h_lo")
        self.xb = sem(tag + "xb")
        self.logits = sem(tag + "logits")
        self.scaled = sem(tag + "scaled")
        self.leaky = sem(tag + "leaky")
        self.tanh = sem(tag + "tanh")
        self.codes = sem(tag + "codes")
        self.codes_kept = sem(tag + "codes_kept")
        self.mask0 = sem(tag + "mask0")
        self.hi0 = sem(tag + "hi0")
        self.lo0 = sem(tag + "lo0")
        self.agg0 = sem(tag + "agg0")
        self.resid0 = sem(tag + "resid0")
        self.stats0 = sem(tag + "stats0")
        self.moments0 = sem(tag + "moments0")
        self.var0 = sem(tag + "var0")
        self.rstd0 = sem(tag + "rstd0")
        self.x1 = sem(tag + "x1")
        self.x1T = sem(tag + "x1T")
        self.x1T_hi = sem(tag + "x1T_hi")
        self.x1T_lo = sem(tag + "x1T_lo")
        self.proj = sem(tag + "proj")
        self.sd = sem(tag + "sd")
        self.scale = sem(tag + "scale")
        self.H_hi = sem(tag + "H_hi")
        self.H_lo = sem(tag + "H_lo")
        self.ones_hi = sem(tag + "ones_hi")
        self.ones_lo = sem(tag + "ones_lo")
        self.squares = sem(tag + "squares")
        self.range_seen = sem(tag + "range_seen")
        self.E = sem(tag + "E")
        self.spread = sem(tag + "spread")
        self.G = sem(tag + "G")
        self.mask1 = sem(tag + "mask1")
        self.hi1 = sem(tag + "hi1")
        self.lo1 = sem(tag + "lo1")
        self.agg1 = sem(tag + "agg1")
        self.rowsum = sem(tag + "rowsum")
        self.rinv = sem(tag + "rinv")
        self.elu_exp = sem(tag + "elu_exp")
        self.relu = sem(tag + "relu")
        self.elu = sem(tag + "elu")
        self.resid1 = sem(tag + "resid1")
        self.stats1 = sem(tag + "stats1")
        self.moments1 = sem(tag + "moments1")
        self.var1 = sem(tag + "var1")
        self.rstd1 = sem(tag + "rstd1")
        self.shift1 = sem(tag + "shift1")
        self.y = sem(tag + "y")
        if general:
            self.plus1 = sem(tag + "plus1")
            self.gx = sem(tag + "gx")
            self.g_hi = sem(tag + "g_hi")
            self.g_lo = sem(tag + "g_lo")
            self.picked = sem(tag + "picked")
            self.summed = sem(tag + "summed")
            self.pair = sem(tag + "pair")
            self.leaky1 = sem(tag + "leaky1")
            self.exp1 = sem(tag + "exp1")
        else:
            self.codes_watched = sem(tag + "codes_watched")
            self.watch_kept = sem(tag + "watch_kept")
            self.mask1_first = sem(tag + "mask1_first")
            self.hi1_first = sem(tag + "hi1_first")
            self.lo1_first = sem(tag + "lo1_first")
            self.mirror = sem(tag + "mirror")
            self.mirror_used = sem(tag + "mirror_used")


def two_graph_layers(nc, x, adj, a0, a1, a2, a3, bias, W, a, out):
    B, N, D = x.shape
    NT = N // P
    KD = D // P
    HC = D + 2
    KINDS = 4
    XT_STEP = {1: 0, 2: 1, 4: 2, 5: 3}
    ACT_CODES = 6
    EARLY = 4
    EDGE = NT // 2

    ROWS = [7, 6, 5, 0, 1, 2, 3, 4]
    CHUNKS = []
    for J in ROWS:
        n = NT - J
        cut = J + (n + 1) // 2 if n > 4 else NT
        CHUNKS.append((J, J, cut))
        if cut < NT:
            CHUNKS.append((J, cut, NT))
    NCH = len(CHUNKS)
    ROW_END = {J: max(k for k in range(NCH) if CHUNKS[k][0] == J) + 1 for J in ROWS}
    MIRRORS = []
    for t in range(NT):
        for j in range(t + 1, NT, 4):
            MIRRORS.append((t, j, min(j + 4, NT)))
    NM = len(MIRRORS)

    x_v = x.rearrange("b (t p) d -> b p t d", p=P)
    adj_v = adj.rearrange("b (t p) j -> b t p j", p=P)
    out_v = out.rearrange("b (t p) d -> b t p d", p=P)

    ctx = ExitStack()
    with ctx:
        def sb(name, shape, dt=FP32):
            return ctx.enter_context(nc.sbuf_tensor(name, shape, dt))

        def bank(name):
            return ctx.enter_context(nc.psum_tensor(name, [P, 512], FP32))

        def sem(name):
            return ctx.enter_context(nc.semaphore(name))

        ident = sb("ident", [P, P])
        ident_bf = sb("ident_bf", [P, P], BF16)
        ones_col = sb("ones_col", [P, 1])
        neg_half = sb("neg_half", [P, 1])
        eps_col = sb("eps_col", [P, 1])
        a_col = sb("a_col", [P, KINDS, KD])
        bias_bc = sb("bias_bc", [P, D])
        W_hi = sb("W_hi", [P, KD, HC], FP32R)
        W_lo = sb("W_lo", [P, KD, HC], FP32R)
        x_raw = sb("x_raw", [P, NT, D])
        xb = sb("xb", [P, NT, D])
        h_hi = sb("h_hi", [P, NT, D], FP32R)
        h_lo = sb("h_lo", [P, NT, D], FP32R)
        hT_hi = sb("hT_hi", [P, KD, N], FP32R)
        hT_lo = sb("hT_lo", [P, KD, N], FP32R)
        gT_hi = sb("gT_hi", [P, KD, N], FP32R)
        gT_lo = sb("gT_lo", [P, KD, N], FP32R)
        score = sb("score", [P, NT // 2, N + N // 2])
        code_nat = sb("code_nat", [P, 4, N], BF16)
        codeT = sb("codeT", [P, NT, N], BF16)
        watch_junk = sb("watch_junk", [P, N], BF16)
        watch_sum = sb("watch_sum", [P, NT])
        watch_max = sb("watch_max", [P, NT])
        coef = sb("coef", [P, 4, N])
        coef_hi = sb("coef_hi", [P, 4, NT, P], FP32R)
        coef_lo = sb("coef_lo", [P, 4, NT, P], FP32R)
        resid = sb("resid", [P, 2, D])
        stats = sb("stats", [P, 2, 6])
        moments = sb("moments", [P, 2, 2])
        var_eps = sb("var_eps", [P, 2, 1])
        rstd = sb("rstd", [P, 2, 1])
        neg_mean = sb("neg_mean", [P, 2, 1])
        shift = sb("shift", [P, 2, 1])
        zero_col = sb("zero_col", [P, 1])
        x1 = sb("x1", [P, NT, D])
        x1T_hi = sb("x1T_hi", [P, 2, KD, P], FP32R)
        x1T_lo = sb("x1T_lo", [P, 2, KD, P], FP32R)
        H_hi = sb("H_hi", [P, NT, HC], FP32R)
        H_lo = sb("H_lo", [P, NT, HC], FP32R)
        sd = sb("sd", [P, NT, 2])
        sd_sq = sb("sd_sq", [P, NT, 2])
        watch_range = sb("watch_range", [P, NT, 2])
        scale_col = sb("scale_col", [P, NT])
        E_col = sb("E_col", [P, NT])
        G = sb("G", [P, N])
        rowsum = sb("rowsum", [P, 2, 1])
        rinv = sb("rinv", [P, 2, 1])
        eluE = sb("eluE", [P, 2, D])
        reluP = sb("reluP", [P, 2, D])
        flag_parts = sb("flag_parts", [P, 3])
        flag_f = sb("flag_f", [P, 1])
        flag_i = sb("flag_i", [1, 1], INT32)

        lg_bank = [bank(f"lg_bank{i}") for i in range(2)]
        acc_bank = [bank(f"acc_bank{i}") for i in range(2)]
        tr_bank = [bank(f"tr_bank{i}") for i in range(2)]
        xt_bank = bank("xt_bank")
        hh_bank = bank("hh_bank")

        W_ext = score[:, 2, 0:KD * HC].rearrange("p (c n) -> p c n", c=KD)
        a_bc = score[:, 3, 0:2 * D]
        gx = score[:, 1, 0:KD * P].rearrange("p (c i) -> p c i", c=KD)
        spread_bank = hh_bank[:, 512 - P:512]

        F = Signals(sem, "f_", False)
        GEN = Signals(sem, "g_", True)
        weights_loaded = sem("weights_loaded")
        ident_made = sem("ident_made")
        consts_made = sem("consts_made")
        setup_step = sem("setup_step")
        weights_ready = sem("weights_ready")
        dve_past = sem("dve_past")
        sp_past = sem("sp_past")
        flag_step = sem("flag_step")
        flag_summed = sem("flag_summed")
        flag_ready = sem("flag_ready")

        N_WEIGHT_DMAS = KINDS + 3
        LAST = B - 1

        def f32(ap):
            return ap.bitcast(FP32)

        def score_at(J, c0, c1):
            if J < NT // 2:
                return score[:, J, c0 * P:c1 * P]
            return score[:, J - NT // 2, (c0 + NT // 2) * P:(c1 + NT // 2) * P]

        def blocks(ap):
            return ap.rearrange("p (j i) -> p j i", i=P)

        block = ctx.enter_context(nc.Block())

        @block.sync
        def _(sp):
            for k, ak in enumerate((a0, a1, a2, a3)):
                with nc.allow_non_contiguous_dma(reason="one column of 256 values"):
                    sp.dma_start(a_col[:, k, :], ak.rearrange("(c p) o -> p (c o)", p=P)).then_inc(weights_loaded, 16)
            sp.dma_start(W_ext[:, :, 0:D], W.rearrange("(c p) o -> p c o", p=P)).then_inc(weights_loaded, 16)
            sp.dma_start(bias_bc[:, :], bias.partition_broadcast(P)).then_inc(weights_loaded, 16)
            sp.dma_start(a_bc[:, :], a[0, :].partition_broadcast(P)).then_inc(weights_loaded, 16)

            def load_x(S, b):
                sp.dma_start(x_raw[:, :, :], x_v[b, :, :, :]).then_inc(S.x_loaded, 16)

            def store(S, b, t):
                sp.wait_ge(S.y, NT * b + t + 1)
                sp.sem_inc(sp_past, 1)
                sp.dma_start(out_v[b, t, :, :], x1[:, t, :]).then_inc(S.out_stored[t if S is F else 0], 16)

            def graph(b, loads):
                for t in range(NT):
                    if loads and t == 2:
                        for made, count in ((F.xb, NT * b + 2 * NT), (F.xT, 4 * b + 8), (F.h_lo, 4 * b + 8)):
                            sp.wait_ge(made, count)
                            sp.sem_inc(sp_past, 1)
                        load_x(F, b + 2)
                    store(F, b, t)

            load_x(F, 0)
            sp.wait_ge(F.h_lo, 4)
            sp.wait_ge(F.xb, NT)
            sp.wait_ge(F.xT, 4)
            sp.sem_inc(sp_past, 1)
            load_x(F, 1)
            with sp.Fori(0, LAST - 1) as b:
                graph(b, True)
            graph(LAST - 1, False)
            graph(LAST, False)
            for s in F.out_stored:
                sp.wait_ge(s, 16 * B)

            sp.wait_ge(flag_ready, 1)
            flag = sp.value_load(flag_i[0:1, 0:1], min_val=0, max_val=512)
            with sp.If(flag > 0):
                with sp.Fori(0, B) as b:
                    load_x(GEN, b)
                    for t in range(NT):
                        store(GEN, b, t)
                    sp.wait_ge(GEN.out_stored[0], 16 * NT * (b + 1))
                    sp.sem_inc(sp_past, 1)

        @block.gpsimd
        def _(pool):
            nc.gpsimd.memset(ident[:, :], 0.0).then_inc(ident_made, 1)
            nc.gpsimd.memset(ident_bf[:, :], 0.0).then_inc(ident_made, 1)
            nc.gpsimd.memset(ones_col[:, :], 1.0).then_inc(consts_made, 1)
            nc.gpsimd.memset(neg_half[:, :], -0.5).then_inc(consts_made, 1)
            nc.gpsimd.memset(eps_col[:, :], EPS).then_inc(consts_made, 1)
            nc.gpsimd.memset(zero_col[:, :], 0.0).then_inc(consts_made, 1)
            pool.wait_ge(ident_made, 2)
            for m in (ident, ident_bf):
                nc.gpsimd.affine_select(out=m[:, :], in_=m[:, :], compare_op=ALU.not_equal, fill=1.0, base=0,
                                        pattern=[[-1, P]], channel_multiplier=1).then_inc(ident_made, 1)

            def load_adj(S, b, t, first):
                if not first:
                    pool.wait_ge(S.codes, NT * b + t - 3)
                pool.dma_start(code_nat[:, t % 4, :], adj_v[b, t, :, :]).then_inc(S.adj_loaded[t % 4], 16)

            def low_x(S, b, c):
                pool.wait_ge(S.h_hi, 4 * b + c + 1)
                nc.gpsimd.tensor_tensor(h_lo[:, 2 * c:2 * c + 2, :], x_raw[:, 2 * c:2 * c + 2, :],
                                        f32(h_hi[:, 2 * c:2 * c + 2, :]), ALU.subtract).then_inc(S.h_lo, 1)

            def add_bias(S, b, t):
                nc.gpsimd.tensor_tensor(xb[:, t, :], x_raw[:, t, :], bias_bc[:, :], ALU.add).then_inc(S.xb, 1)

            def low0(S, b, t):
                pool.wait_ge(S.hi0, NT * b + t + 1)
                nc.gpsimd.tensor_tensor(coef_lo[:, t % 4, :, :], blocks(coef[:, t % 4, :]),
                                        f32(coef_hi[:, t % 4, :, :]), ALU.subtract).then_inc(S.lo0, 1)

            def low1(S, b, t, j0=0, j1=NT):
                if j1 == NT:
                    pool.wait_ge(S.hi1, NT * b + t + 1)
                else:
                    pool.wait_ge(S.hi1_first, EARLY * b + t + 1)
                nc.gpsimd.tensor_tensor(coef_lo[:, t % 4, j0:j1, :], blocks(coef[:, t % 4, j0 * P:j1 * P]),
                                        f32(coef_hi[:, t % 4, j0:j1, :]),
                                        ALU.subtract).then_inc(S.lo1 if j1 == NT else S.lo1_first, 1)

            def power0(S, b, t):
                pool.wait_ge(S.moments0, NT * b + t + 1)
                nc.gpsimd.tensor_tensor(var_eps[:, t % 2, :], moments[:, t % 2, 1:2], eps_col[:, :],
                                        ALU.add).then_inc(S.var0, 1)
                pool.wait_ge(S.var0, NT * b + t + 1)
                nc.gpsimd.tensor_tensor(rstd[:, t % 2, :], var_eps[:, t % 2, :], neg_half[:, :],
                                        ALU.pow).then_inc(S.rstd0, 1)

            def power1(S, b, t):
                pool.wait_ge(S.moments1, NT * b + t + 1)
                nc.gpsimd.tensor_tensor(neg_mean[:, t % 2, :], zero_col[:, :], moments[:, t % 2, 0:1], ALU.subtract)
                nc.gpsimd.tensor_tensor(var_eps[:, t % 2, :], moments[:, t % 2, 1:2], eps_col[:, :],
                                        ALU.add).then_inc(S.var1, 1)
                pool.wait_ge(S.var1, NT * b + t + 1)
                nc.gpsimd.tensor_tensor(rstd[:, t % 2, :], var_eps[:, t % 2, :], neg_half[:, :],
                                        ALU.pow).then_inc(S.rstd1, 1)
                pool.wait_ge(S.rstd1, NT * b + t + 1)
                nc.gpsimd.tensor_tensor(shift[:, t % 2, :], neg_mean[:, t % 2, :], rstd[:, t % 2, :],
                                        ALU.mult).then_inc(S.shift1, 1)

            def pair(b, t):
                if t == 0:
                    pool.wait_ge(GEN.E, NT * b + NT)
                    pool.wait_ge(GEN.G, NT * b + NT)
                s_b = G[:, t * P:(t + 1) * P].unsqueeze(1).broadcast_to([P, NT, P])
                d_b = E_col[:, :].unsqueeze(2).broadcast_to([P, NT, P])
                nc.gpsimd.tensor_tensor(blocks(coef[:, t % 4, :]), s_b, d_b, ALU.add).then_inc(GEN.pair, 1)

            def next_bias(b, u):
                pool.wait_ge(F.resid0, NT * b + u + 1)
                add_bias(F, b + 1, u)

            def graph(b, nxt):
                for t in range(NT + 1):
                    if t >= 1:
                        power0(F, b, t - 1)
                    if nxt and t >= 2:
                        if t == 2:
                            pool.wait_ge(F.x_loaded, 16 * (b + 2))
                        next_bias(b, t - 2)
                    if 1 <= t and t + 3 < NT:
                        low0(F, b, t + 3)
                    if t >= 7:
                        low1(F, b, t - 7, 0, EDGE)
                    if nxt and t >= 5:
                        load_adj(F, b + 1, t - 5, False)
                low1(F, b, 2, 0, EDGE)
                if nxt:
                    next_bias(b, NT - 1)
                low1(F, b, 3, 0, EDGE)
                for t in range(EARLY):
                    low1(F, b, t, EDGE, NT)
                if nxt:
                    for t in range(4, 7):
                        load_adj(F, b + 1, t, False)
                    low_x(F, b + 1, 0)
                for t in range(NT + 1):
                    if t >= 2:
                        power1(F, b, t - 2)
                    if nxt:
                        if t == 0:
                            for c in range(1, 4):
                                low_x(F, b + 1, c)
                        if t == 2:
                            load_adj(F, b + 1, 7, False)
                    if 1 <= t and t + 3 < NT:
                        low1(F, b, t + 3)
                    elif t + 3 >= NT and nxt:
                        low0(F, b + 1, t + 3 - NT)
                power1(F, b, NT - 1)

            pool.wait_ge(consts_made, 4)
            pool.wait_ge(F.x_loaded, 16)
            pool.wait_ge(weights_loaded, 16 * N_WEIGHT_DMAS)
            for t in range(4):
                load_adj(F, 0, t, True)
            for t in range(NT):
                add_bias(F, 0, t)
            for c in range(4):
                low_x(F, 0, c)
            for t in range(4, NT):
                load_adj(F, 0, t, False)
            for t in range(4):
                low0(F, 0, t)
            with pool.Fori(0, LAST) as b:
                graph(b, True)
            graph(LAST, False)

            pool.wait_ge(flag_ready, 1)
            flag = pool.value_load(flag_i[0:1, 0:1], min_val=0, max_val=512)
            with pool.If(flag > 0):
                with pool.Fori(0, B) as b:
                    pool.wait_ge(GEN.x_loaded, 16 * b + 16)
                    for t in range(NT):
                        add_bias(GEN, b, t)
                    for c in range(4):
                        low_x(GEN, b, c)
                    for t in range(NT):
                        load_adj(GEN, b, t, t < 4)
                        low0(GEN, b, t)
                        power0(GEN, b, t)
                    for t in range(NT):
                        pair(b, t)
                        low1(GEN, b, t)
                        power1(GEN, b, t)
                    pool.wait_ge(GEN.out_stored[0], 16 * NT * (b + 1))

        @block.scalar
        def _(act):
            def high_xT(S, b, c, general):
                act.wait_ge(S.xT, 4 * b + c + 1)
                if not general:
                    if not isinstance(b, int) or b > 0:
                        act.wait_ge(S.logits, NCH * b)
                cols = slice((NT - 2 * c - 2) * P, (NT - 2 * c) * P)
                xt = lg_bank[c % 2][:, :].rearrange("p (c i) -> p c i", c=KD)
                ins = nc.scalar.activation(hT_hi[:, :, cols], xt, ACT.Copy)
                if not general:
                    for dt in range(KD):
                        ins = nc.scalar.activation(gT_hi[:, dt, cols], xt[:, dt, :], ACT.Copy,
                                                   scale=a_col[:, 0, dt:dt + 1])
                ins.then_inc(S.xT_hi, 1)

            def high_x(S, b, c):
                if c == 0:
                    act.wait_ge(S.x_loaded, 16 * b + 16)
                    if S is F and (not isinstance(b, int) or b > 0):
                        act.wait_ge(S.agg0, NT * b)
                nc.scalar.activation(h_hi[:, 2 * c:2 * c + 2, :], x_raw[:, 2 * c:2 * c + 2, :],
                                     ACT.Copy).then_inc(S.h_hi, 1)

            def scale_scores(b, k):
                J, c0, c1 = CHUNKS[k]
                act.wait_ge(F.logits, NCH * b + k + 1)
                if k == 0:
                    if isinstance(b, int) and b == 0:
                        act.wait_ge(weights_ready, 1)
                    else:
                        act.wait_ge(F.mask0, NT * b)
                nc.scalar.activation(score_at(J, c0, c1), lg_bank[k % 2][:, 0:(c1 - c0) * P], ACT.Copy,
                                     scale=SLOPE).then_inc(F.scaled, 1)

            def scale_row(b, J):
                for k in range(NCH):
                    if CHUNKS[k][0] == J:
                        scale_scores(b, k)

            def tanh_row(b, J):
                act.wait_ge(F.leaky, NCH * b + ROW_END[J])
                nc.scalar.activation(score_at(J, J, NT), score_at(J, J, NT), ACT.Tanh,
                                     scale=0.5).then_inc(F.tanh, 1)

            def keep_codes(S, b, t, prev):
                act.wait_ge(S.codes, NT * b + t + 1)
                if prev:
                    act.wait_ge(S.mask1, NT * b + t + 1 - NT)
                    act.wait_ge(S.codes_watched, NT * b + t + 1 - NT)
                nc.scalar.activation(codeT[:, t, :], tr_bank[t % 2][:, :].bitcast(BF16),
                                     ACT.Copy).then_inc(S.codes_kept, 1)

            def watch_codes(b, t):
                act.wait_ge(F.codes_kept, NT * b + t + 1)
                if t == 0 and not (isinstance(b, int) and b == 0):
                    act.wait_ge(F.watch_kept, b)
                if not (isinstance(b, int) and b == 0 and t == 0):
                    act.wait_ge(F.codes_watched, NT * b + t)
                nc.scalar.activation(watch_junk[:, :], codeT[:, t, :], ACT.Square, bias=neg_half[:, :],
                                     accum_out=watch_sum[:, t:t + 1]).then_inc(F.codes_watched, 1)

            def high0(S, b, t, prev):
                act.wait_ge(S.mask0, NT * b + t + 1)
                if t >= 4:
                    act.wait_ge(S.agg0, NT * b + t - 3)
                elif prev:
                    act.wait_ge(S.agg1, NT * b + t - 3)
                nc.scalar.activation(coef_hi[:, t % 4, :, :], blocks(coef[:, t % 4, :]),
                                     ACT.Copy).then_inc(S.hi0, 1)

            def high1(S, b, t, j0=0, j1=NT):
                if j1 == NT:
                    act.wait_ge(S.mask1, NT * b + t + 1)
                else:
                    act.wait_ge(S.mask1_first, EARLY * b + t + 1)
                if t >= 4:
                    act.wait_ge(S.agg1, NT * b + t - 3)
                else:
                    act.wait_ge(S.agg0, NT * b + t + 5)
                nc.scalar.activation(coef_hi[:, t % 4, j0:j1, :], blocks(coef[:, t % 4, j0 * P:j1 * P]),
                                     ACT.Copy).then_inc(S.hi1 if j1 == NT else S.hi1_first, 1)

            def high_x1T(S, b, t, prev):
                act.wait_ge(S.x1T, NT * b + t + 1)
                if t >= 2 or prev:
                    act.wait_ge(S.proj, NT * b + t - 1)
                nc.scalar.activation(x1T_hi[:, t % 2, :, :],
                                     xt_bank[:, 0:D].rearrange("p (c i) -> p c i", c=KD),
                                     ACT.Copy).then_inc(S.x1T_hi, 1)

            def make_G(S, b, t, general):
                nc.scalar.activation(G[:, t * P:(t + 1) * P], spread_bank, ACT.Copy if general else ACT.Exp,
                                     scale=1.0 if general else 1.0 - SLOPE).then_inc(S.G, 1)

            def high_H(S, b, t, prev, general):
                act.wait_ge(S.proj, NT * b + t + 1)
                if prev and t == 0:
                    act.wait_ge(S.agg1, NT * b)
                nc.scalar.activation(scale_col[:, t:t + 1], hh_bank[:, D:D + 1], ACT.Exp,
                                     scale=0.0 if general else -SLOPE).then_inc(S.scale, 1)
                nc.scalar.activation(E_col[:, t:t + 1], hh_bank[:, D:D + 1], ACT.Copy if general else ACT.Exp,
                                     scale=1.0 if general else SLOPE - 1.0).then_inc(S.E, 1)
                if t >= 1:
                    make_G(S, b, t - 1, general)
                nc.scalar.activation(sd[:, t, :], hh_bank[:, D:D + 2], ACT.Copy).then_inc(S.sd, 1)
                act.wait_ge(S.scale, NT * b + t + 1)
                nc.scalar.activation(H_hi[:, t, 0:D], hh_bank[:, 0:D], ACT.Copy,
                                     scale=scale_col[:, t:t + 1]).then_inc(S.H_hi, 1)

            def ends_H(S, b):
                nc.scalar.activation(H_hi[:, :, D], scale_col[:, :], ACT.Copy).then_inc(S.ones_hi, 1)

            def last_G(S, b, general):
                act.wait_ge(S.spread, b + 1)
                make_G(S, b, NT - 1, general)

            def elu_parts(S, b, t):
                act.wait_ge(S.rinv, NT * b + t + 1)
                if t >= 2 or S is F and (not isinstance(b, int) or b > 0):
                    act.wait_ge(S.elu, NT * b + t - 1)
                nc.scalar.activation(eluE[:, t % 2, :], acc_bank[t % 2][:, 0:D], ACT.Exp,
                                     scale=rinv[:, t % 2, :]).then_inc(S.elu_exp, 1)
                nc.scalar.activation(reluP[:, t % 2, :], acc_bank[t % 2][:, 0:D], ACT.Relu,
                                     scale=rinv[:, t % 2, :]).then_inc(S.relu, 1)

            def norm1(S, b, t):
                act.wait_ge(S.shift1, NT * b + t + 1)
                nc.scalar.activation(x1[:, t, :], resid[:, t % 2, :], ACT.Identity, bias=shift[:, t % 2, :],
                                     scale=rstd[:, t % 2, :]).then_inc(S.y, 1)

            def graph(b, prev, nxt):
                for t in range(NT + 1):
                    if t >= 3:
                        high_H(F, b, t - 3, prev, False)
                    if t >= 2:
                        high_x1T(F, b, t - 2, prev)
                    if nxt and t in XT_STEP:
                        high_xT(F, b + 1, XT_STEP[t], False)
                    if t < 6:
                        watch_codes(b, t)
                    if 1 <= t and t + 3 < NT:
                        high0(F, b, t + 3, prev)
                    if t == 1 and prev:
                        norm1(F, b - 1, NT - 1)
                    if nxt and 6 <= t:
                        scale_scores(b + 1, t - 6)
                    if t >= 7:
                        high1(F, b, t - 7, 0, EDGE)
                    if t in (6, 7):
                        watch_codes(b, t)
                high_H(F, b, 6, prev, False)
                if nxt:
                    scale_scores(b + 1, 3)
                high_x1T(F, b, 7, prev)
                high1(F, b, 2, 0, EDGE)
                if nxt:
                    scale_scores(b + 1, 4)
                high_H(F, b, 7, prev, False)
                ends_H(F, b)
                high1(F, b, 3, 0, EDGE)
                if nxt:
                    scale_scores(b + 1, 5)
                high1(F, b, 0, EDGE, NT)
                high1(F, b, 1, EDGE, NT)
                if nxt:
                    scale_scores(b + 1, 6)
                    keep_codes(F, b + 1, 0, True)
                high1(F, b, 2, EDGE, NT)
                last_G(F, b, False)
                high1(F, b, 3, EDGE, NT)
                if nxt:
                    scale_scores(b + 1, 7)
                    keep_codes(F, b + 1, 1, True)
                    high_x(F, b + 1, 0)
                    high_x(F, b + 1, 1)
                    keep_codes(F, b + 1, 2, True)
                for t in range(NT + 1):
                    if t >= 1:
                        elu_parts(F, b, t - 1)
                    if nxt and t == 0:
                        scale_scores(b + 1, 8)
                    if nxt and 1 <= t < 3:
                        scale_row(b + 1, 2 + t)
                    if 1 <= t and t + 3 < NT:
                        high1(F, b, t + 3)
                    elif t + 3 >= NT and nxt:
                        high0(F, b + 1, t + 3 - NT, True)
                    if nxt:
                        if t + 3 < ACT_CODES:
                            keep_codes(F, b + 1, t + 3, True)
                        if t == 0:
                            high_x(F, b + 1, 2)
                            high_x(F, b + 1, 3)
                        if 1 <= t:
                            tanh_row(b + 1, t - 1)
                    if t >= 2:
                        norm1(F, b, t - 2)

            act.wait_ge(weights_loaded, 16 * N_WEIGHT_DMAS)
            for c in range(4):
                high_xT(F, 0, c, False)
                high_x(F, 0, c)
            for J in ROWS:
                scale_row(0, J)
            for t in range(NT):
                keep_codes(F, 0, t, False)
            for J in range(NT):
                tanh_row(0, J)
            act.wait_ge(consts_made, 4)
            for t in range(4):
                high0(F, 0, t, False)
            graph(0, False, True)
            with act.Fori(1, LAST) as b:
                graph(b, True, True)
            graph(LAST, True, False)
            norm1(F, LAST, NT - 1)

            act.wait_ge(flag_ready, 1)
            flag = act.value_load(flag_i[0:1, 0:1], min_val=0, max_val=512)
            with act.If(flag > 0):
                with act.Fori(0, B) as b:
                    for c in range(4):
                        high_xT(GEN, b, c, True)
                        high_x(GEN, b, c)
                    for t in range(NT):
                        keep_codes(GEN, b, t, False)
                        for k in range(KINDS):
                            n = KINDS * (NT * b + t) + k
                            act.wait_ge(GEN.logits, n + 1)
                            nc.scalar.activation(score[:, 0, 0:512], lg_bank[0][:, :], ACT.Copy, scale=SLOPE)
                            nc.scalar.activation(score[:, 0, 512:N], lg_bank[1][:, :], ACT.Copy,
                                                 scale=SLOPE).then_inc(GEN.scaled, 1)
                            act.wait_ge(GEN.leaky, n + 1)
                            nc.scalar.activation(score[:, 0, 0:N], score[:, 0, 0:N], ACT.Tanh,
                                                 scale=0.5).then_inc(GEN.tanh, 1)
                        high0(GEN, b, t, False)
                        high_x1T(GEN, b, t, False)
                        high_H(GEN, b, t, False, True)
                    ends_H(GEN, b)
                    last_G(GEN, b, True)
                    for t in range(NT):
                        act.wait_ge(GEN.leaky1, NT * b + t + 1)
                        nc.scalar.activation(coef[:, t % 4, :], coef[:, t % 4, :], ACT.Exp,
                                             scale=-1.0).then_inc(GEN.exp1, 1)
                        high1(GEN, b, t)
                        elu_parts(GEN, b, t)
                        norm1(GEN, b, t)
                    act.wait_ge(GEN.out_stored[0], 16 * NT * (b + 1))

        @block.vector
        def _(dve):
            nc.vector.memset(watch_max[:, :], 0.0).then_inc(setup_step, 1)
            nc.vector.memset(watch_range[:, :, :], 0.0).then_inc(setup_step, 1)
            nc.vector.memset(sd_sq[:, :, :], 0.0).then_inc(setup_step, 1)
            dve.wait_ge(setup_step, 3)
            nc.vector.tensor_copy(H_hi[:, :, D + 1], sd_sq[:, :, 0]).then_inc(setup_step, 1)
            nc.vector.tensor_copy(H_lo[:, :, D + 1], sd_sq[:, :, 0]).then_inc(setup_step, 1)
            dve.wait_ge(weights_loaded, 16 * N_WEIGHT_DMAS)
            steps = 5
            for which, col in ((1, D), (0, D + 1)):
                for dt in range(KD):
                    nc.vector.tensor_tensor(reluP[:, 0, :], W_ext[:, dt, 0:D], a_bc[:, which * D:(which + 1) * D],
                                            ALU.mult).then_inc(setup_step, 1)
                    dve.wait_ge(setup_step, steps + 1)
                    nc.vector.tensor_reduce(W_ext[:, dt, col:col + 1], reluP[:, 0, :], AX.X,
                                            ALU.add).then_inc(setup_step, 1)
                    dve.wait_ge(setup_step, steps + 2)
                    steps += 2
            nc.vector.tensor_copy(W_hi[:, :, :], W_ext[:, :, :]).then_inc(setup_step, 1)
            dve.wait_ge(setup_step, steps + 1)
            nc.vector.tensor_tensor(W_lo[:, :, :], W_ext[:, :, :], f32(W_hi[:, :, :]),
                                    ALU.subtract).then_inc(weights_ready, 1)

            def low_xT(S, b, c, general):
                dve.wait_ge(S.xT_hi, 4 * b + c + 1)
                cols = slice((NT - 2 * c - 2) * P, (NT - 2 * c) * P)
                xt = lg_bank[c % 2][:, :].rearrange("p (c i) -> p c i", c=KD)
                ins = nc.vector.tensor_tensor(hT_lo[:, :, cols], xt, f32(hT_hi[:, :, cols]), ALU.subtract)
                if not general:
                    for dt in range(KD):
                        ins = nc.vector.scalar_tensor_tensor(gT_lo[:, dt, cols], xt[:, dt, :],
                                                             a_col[:, 0, dt:dt + 1], f32(gT_hi[:, dt, cols]),
                                                             ALU.mult, ALU.subtract)
                ins.then_inc(S.xT_lo, 1)

            def leaky_scores(b, k):
                J, c0, c1 = CHUNKS[k]
                dve.wait_ge(F.scaled, NCH * b + k + 1)
                nc.vector.tensor_tensor(score_at(J, c0, c1), lg_bank[k % 2][:, 0:(c1 - c0) * P],
                                        score_at(J, c0, c1), ALU.max).then_inc(F.leaky, 1)

            def leaky_row(b, J):
                for k in range(NCH):
                    if CHUNKS[k][0] == J:
                        leaky_scores(b, k)

            def keep_watch(b, prev):
                dve.wait_ge(F.codes_watched, NT * b + NT)
                if prev:
                    dve.wait_ge(F.watch_kept, b)
                nc.vector.tensor_tensor(watch_max[:, :], watch_max[:, :], watch_sum[:, :],
                                        ALU.max).then_inc(F.watch_kept, 1)

            def keep_codes(b, t):
                dve.wait_ge(F.codes, NT * b + t + 1)
                dve.wait_ge(F.codes_kept, NT * b + t)
                dve.wait_ge(F.mask1, NT * b + t + 1 - NT)
                dve.wait_ge(F.codes_watched, NT * b + t + 1 - NT)
                nc.vector.tensor_copy(codeT[:, t, :],
                                      tr_bank[t % 2][:, :].bitcast(BF16)).then_inc(F.codes_kept, 1)

            def mask0(b, t, prev):
                dve.wait_ge(F.tanh, NT * b + t + 1)
                dve.wait_ge(F.codes_kept, NT * b + t + 1)
                if t >= 4:
                    dve.wait_ge(F.lo0, NT * b + t - 3)
                elif prev:
                    dve.wait_ge(F.lo1, NT * b + t - 3)
                for m, (tt, j0, j1) in enumerate(MIRRORS):
                    if tt == t:
                        dve.wait_ge(F.mirror, NM * b + m + 1)
                        nc.vector.scalar_tensor_tensor(
                            coef[:, t % 4, j0 * P:j1 * P], tr_bank[m % 2][:, 0:(j1 - j0) * P], 1.0,
                            codeT[:, t, j0 * P:j1 * P], ALU.add, ALU.mult).then_inc(F.mirror_used, 1)
                for j0, j1 in ((0, min(t + 1, NT // 2)), (NT // 2, t + 1)):
                    if j0 < j1:
                        at = t * P + j0 * P
                        ins = nc.vector.scalar_tensor_tensor(
                            blocks(coef[:, t % 4, j0 * P:j1 * P]), score[:, 0:j1 - j0, at:at + P], 1.0,
                            blocks(codeT[:, t, j0 * P:j1 * P]), ALU.add, ALU.mult)
                ins.then_inc(F.mask0, 1)

            def residual0(S, b, t, prev):
                if t >= 2:
                    dve.wait_ge(S.x1, NT * b + t - 1)
                elif prev:
                    dve.wait_ge(S.y, NT * b + t - 1)
                dve.wait_ge(S.agg0, NT * b + t + 1)
                if t == 0:
                    dve.wait_ge(S.xb, NT * b + NT)
                nc.vector.scalar_tensor_tensor(resid[:, t % 2, :], acc_bank[t % 2][:, 0:D], 0.5, xb[:, t, :],
                                               ALU.mult, ALU.add).then_inc(S.resid0, 1)
                dve.wait_ge(S.resid0, NT * b + t + 1)
                nc.vector.bn_stats(stats[:, t % 2, :], resid[:, t % 2, :]).then_inc(S.stats0, 1)
                dve.wait_ge(S.stats0, NT * b + t + 1)
                dve.sem_inc(dve_past, 1)
                nc.vector.bn_aggr(moments[:, t % 2, :], stats[:, t % 2, :]).then_inc(S.moments0, 1)

            def norm0(S, b, t, prev):
                dve.wait_ge(S.rstd0, NT * b + t + 1)
                if prev:
                    dve.wait_ge(S.out_stored[t], 16 * b)
                nc.vector.tensor_scalar(x1[:, t, :], resid[:, t % 2, :], moments[:, t % 2, 0:1],
                                        rstd[:, t % 2, :], ALU.subtract, ALU.mult).then_inc(S.x1, 1)

            def low_x1T(S, b, t):
                dve.wait_ge(S.x1T_hi, NT * b + t + 1)
                nc.vector.tensor_tensor(x1T_lo[:, t % 2, :, :],
                                        xt_bank[:, 0:D].rearrange("p (c i) -> p c i", c=KD),
                                        f32(x1T_hi[:, t % 2, :, :]), ALU.subtract).then_inc(S.x1T_lo, 1)

            def low_H(S, b, t):
                dve.wait_ge(S.H_hi, NT * b + t + 1)
                nc.vector.scalar_tensor_tensor(H_lo[:, t, 0:D], hh_bank[:, 0:D], scale_col[:, t:t + 1],
                                               f32(H_hi[:, t, 0:D]), ALU.mult, ALU.subtract).then_inc(S.H_lo, 1)

            def ends_H(S, b, prev):
                if prev:
                    dve.wait_ge(S.range_seen, b)
                dve.wait_ge(S.ones_hi, b + 1)
                nc.vector.tensor_tensor(H_lo[:, :, D], scale_col[:, :], f32(H_hi[:, :, D]),
                                        ALU.subtract).then_inc(S.ones_lo, 1)
                nc.vector.tensor_tensor(sd_sq[:, :, :], sd[:, :, :], sd[:, :, :], ALU.mult).then_inc(S.squares, 1)
                dve.wait_ge(S.squares, b + 1)
                nc.vector.tensor_tensor(watch_range[:, :, :], watch_range[:, :, :], sd_sq[:, :, :],
                                        ALU.max).then_inc(S.range_seen, 1)

            def mask1_pair(b, t, j0=0, j1=NT):
                dve.wait_ge(F.E, NT * b + j1)
                dve.wait_ge(F.G, NT * b + t + 2)
                if t < 4:
                    dve.wait_ge(F.lo0, NT * b + t + 6)
                else:
                    dve.wait_ge(F.lo1, NT * b + t - 2)
                for J in range(j0, j1):
                    ins = nc.vector.scalar_tensor_tensor(
                        coef[:, t % 4:t % 4 + 2, J * P:(J + 1) * P], blocks(G[:, t * P:(t + 2) * P]),
                        E_col[:, J:J + 1], codeT[:, t:t + 2, J * P:(J + 1) * P], ALU.min, ALU.mult)
                ins.then_inc(F.mask1 if j1 == NT else F.mask1_first, 2)

            def row_inverse(S, b, t, prev):
                if t >= 2 or prev:
                    dve.wait_ge(S.rinv, NT * b + t - 1)
                dve.wait_ge(S.agg1, NT * b + t + 1)
                if S is F:
                    nc.vector.tensor_scalar(rowsum[:, t % 2, :], acc_bank[t % 2][:, D:D + 1], LEAST_ROWSUM, None,
                                            ALU.max).then_inc(S.rowsum, 1)
                    dve.wait_ge(S.rowsum, NT * b + t + 1)
                else:
                    nc.vector.tensor_scalar(rowsum[:, t % 2, :], acc_bank[t % 2][:, D:D + 1], 0.0, None,
                                            ALU.is_equal).then_inc(S.rowsum, 1)
                    dve.wait_ge(S.rowsum, 2 * (NT * b + t) + 1)
                    nc.vector.tensor_tensor(rowsum[:, t % 2, :], acc_bank[t % 2][:, D:D + 1], rowsum[:, t % 2, :],
                                            ALU.add).then_inc(S.rowsum, 1)
                    dve.wait_ge(S.rowsum, 2 * (NT * b + t) + 2)
                nc.vector.reciprocal(rinv[:, t % 2, :], rowsum[:, t % 2, :]).then_inc(S.rinv, 1)

            def residual1(S, b, t):
                if t >= 2:
                    dve.wait_ge(S.y, NT * b + t - 1)
                else:
                    dve.wait_ge(S.x1, NT * b + t + 7)
                dve.wait_ge(S.relu, NT * b + t + 1)
                nc.vector.scalar_tensor_tensor(reluP[:, t % 2, :], eluE[:, t % 2, :], 1.0, reluP[:, t % 2, :],
                                               ALU.min, ALU.add).then_inc(S.elu, 1)
                dve.wait_ge(S.elu, NT * b + t + 1)
                nc.vector.scalar_tensor_tensor(resid[:, t % 2, :], reluP[:, t % 2, :], -1.0, x1[:, t, :],
                                               ALU.add, ALU.add).then_inc(S.resid1, 1)
                dve.wait_ge(S.resid1, NT * b + t + 1)
                nc.vector.bn_stats(stats[:, t % 2, :], resid[:, t % 2, :]).then_inc(S.stats1, 1)
                dve.wait_ge(S.stats1, NT * b + t + 1)
                dve.sem_inc(dve_past, 1)
                nc.vector.bn_aggr(moments[:, t % 2, :], stats[:, t % 2, :]).then_inc(S.moments1, 1)

            def graph(b, prev, nxt):
                for t in range(NT + 1):
                    if t >= 1:
                        residual0(F, b, t - 1, prev)
                    if t >= 3:
                        low_H(F, b, t - 3)
                    if t >= 2:
                        low_x1T(F, b, t - 2)
                    if 1 <= t and t + 3 < NT:
                        mask0(b, t + 3, prev)
                    if t == 6:
                        mask1_pair(b, 0, 0, EDGE)
                    if t == 7:
                        mask1_pair(b, 2, 0, EDGE)
                    if nxt and t == 1:
                        low_xT(F, b + 1, XT_STEP[t], False)
                    if t >= 1:
                        norm0(F, b, t - 1, prev)
                    if nxt and t > 1 and t in XT_STEP:
                        low_xT(F, b + 1, XT_STEP[t], False)
                    if nxt and 6 <= t:
                        leaky_scores(b + 1, t - 6)
                low_H(F, b, 6)
                if nxt:
                    leaky_scores(b + 1, 3)
                low_x1T(F, b, 7)
                if nxt:
                    leaky_scores(b + 1, 4)
                low_H(F, b, 7)
                mask1_pair(b, 0, EDGE, NT)
                ends_H(F, b, prev)
                if nxt:
                    leaky_scores(b + 1, 5)
                mask1_pair(b, 2, EDGE, NT)
                if nxt:
                    leaky_scores(b + 1, 6)
                keep_watch(b, prev)
                for t in range(NT + 1):
                    if t >= 1:
                        row_inverse(F, b, t - 1, prev)
                    if t in (0, 2):
                        mask1_pair(b, t + 4)
                    if t + 3 >= NT and nxt:
                        mask0(b + 1, t + 3 - NT, True)
                    if nxt and ACT_CODES <= t + 3 < NT:
                        keep_codes(b + 1, t + 3)
                    if t >= 1:
                        residual1(F, b, t - 1)
                    if nxt and t < 3:
                        leaky_row(b + 1, 2 + t)

            for c in range(4):
                low_xT(F, 0, c, False)
            for J in ROWS:
                leaky_row(0, J)
            for t in range(4):
                mask0(0, t, False)
            graph(0, False, True)
            with dve.Fori(1, LAST) as b:
                graph(b, True, True)
            graph(LAST, True, False)

            dve.wait_ge(F.watch_kept, B)
            dve.wait_ge(F.range_seen, B)
            nc.vector.tensor_reduce(flag_parts[:, 0:1], watch_max[:, :], AX.X, ALU.max).then_inc(flag_step, 1)
            nc.vector.tensor_reduce(flag_parts[:, 1:2], watch_range[:, :, :], AX.XY, ALU.max).then_inc(flag_step, 1)
            dve.wait_ge(flag_step, 2)
            nc.vector.tensor_scalar(flag_parts[:, 0:1], flag_parts[:, 0:1], N / 4 + 1.0, None,
                                    ALU.is_gt).then_inc(flag_step, 1)
            nc.vector.tensor_scalar(flag_parts[:, 2:3], flag_parts[:, 1:2], RANGE_MAX * RANGE_MAX, None,
                                    ALU.is_gt).then_inc(flag_step, 1)
            dve.wait_ge(flag_step, 4)
            nc.vector.tensor_tensor(flag_f[:, :], flag_parts[:, 0:1], flag_parts[:, 2:3],
                                    ALU.add).then_inc(flag_step, 1)
            dve.wait_ge(flag_summed, 1)
            nc.vector.tensor_copy(flag_i[:, :], xt_bank[0:1, 0:1]).then_inc(flag_ready, 1)

            dve.wait_ge(flag_ready, 1)
            flag = dve.value_load(flag_i[0:1, 0:1], min_val=0, max_val=512)
            with dve.If(flag > 0):
                with dve.Fori(0, B) as b:
                    for c in range(4):
                        low_xT(GEN, b, c, True)
                    for t in range(NT):
                        cols = slice(t * P, (t + 1) * P)
                        dve.wait_ge(GEN.xT_lo, 4 * b + 4)
                        if t:
                            dve.wait_ge(GEN.logits, KINDS * (NT * b + t))
                        nc.vector.tensor_tensor(gx[:, :, :], f32(hT_hi[:, :, cols]), f32(hT_lo[:, :, cols]),
                                                ALU.add).then_inc(GEN.gx, 1)
                        dve.wait_ge(GEN.gx, NT * b + t + 1)
                        for k in range(KINDS):
                            n = KINDS * (NT * b + t) + k
                            if k:
                                dve.wait_ge(GEN.logits, n)
                            for dt in range(KD):
                                ins = nc.vector.tensor_scalar(gT_hi[:, dt, 0:P], gx[:, dt, :],
                                                              a_col[:, k, dt:dt + 1], None, ALU.mult)
                            ins.then_inc(GEN.g_hi, 1)
                            dve.wait_ge(GEN.g_hi, n + 1)
                            for dt in range(KD):
                                ins = nc.vector.scalar_tensor_tensor(gT_lo[:, dt, 0:P], gx[:, dt, :],
                                                                     a_col[:, k, dt:dt + 1],
                                                                     f32(gT_hi[:, dt, 0:P]), ALU.mult, ALU.subtract)
                            ins.then_inc(GEN.g_lo, 1)
                            dve.wait_ge(GEN.scaled, n + 1)
                            nc.vector.tensor_tensor(score[:, 0, 0:512], lg_bank[0][:, :], score[:, 0, 0:512],
                                                    ALU.max)
                            nc.vector.tensor_tensor(score[:, 0, 512:N], lg_bank[1][:, :], score[:, 0, 512:N],
                                                    ALU.max).then_inc(GEN.leaky, 1)
                            dve.wait_ge(GEN.tanh, n + 1)
                            nc.vector.tensor_scalar(score[:, 0, 0:N], score[:, 0, 0:N], 1.0, None,
                                                    ALU.add).then_inc(GEN.plus1, 1)
                            dve.wait_ge(GEN.plus1, n + 1)
                            if k == 0:
                                dve.wait_ge(GEN.codes_kept, NT * b + t + 1)
                                if t >= 4:
                                    dve.wait_ge(GEN.lo0, NT * b + t - 3)
                            dst = coef[:, t % 4, :] if k == 0 else score[:, 0, 0:N]
                            nc.vector.scalar_tensor_tensor(dst, codeT[:, t, :], float(k + 1), score[:, 0, 0:N],
                                                           ALU.is_equal, ALU.mult).then_inc(GEN.picked, 1)
                            dve.wait_ge(GEN.picked, n + 1)
                            if k:
                                ins = nc.vector.tensor_tensor(coef[:, t % 4, :], coef[:, t % 4, :],
                                                              score[:, 0, 0:N], ALU.add)
                                ins.then_inc(GEN.mask0 if k == KINDS - 1 else GEN.summed, 1)
                                if k < KINDS - 1:
                                    dve.wait_ge(GEN.summed, 2 * (NT * b + t) + k)
                        residual0(GEN, b, t, False)
                        norm0(GEN, b, t, False)
                        low_x1T(GEN, b, t)
                        low_H(GEN, b, t)
                    ends_H(GEN, b, False)
                    for t in range(NT):
                        dve.wait_ge(GEN.pair, NT * b + t + 1)
                        nc.vector.scalar_tensor_tensor(coef[:, t % 4, :], coef[:, t % 4, :], SLOPE,
                                                       coef[:, t % 4, :], ALU.mult, ALU.max).then_inc(GEN.leaky1, 1)
                        dve.wait_ge(GEN.exp1, NT * b + t + 1)
                        nc.vector.scalar_tensor_tensor(coef[:, t % 4, :], codeT[:, t, :], 0.0, coef[:, t % 4, :],
                                                       ALU.not_equal, ALU.mult).then_inc(GEN.mask1, 1)
                        row_inverse(GEN, b, t, False)
                        residual1(GEN, b, t)
                    dve.wait_ge(GEN.out_stored[0], 16 * NT * (b + 1))

        @block.tensor
        def _(pe):
            def split_products(dst, lhs_hi, lhs_lo, rhs_hi, rhs_lo, first, last):
                nc.tensor.matmul(dst, lhs_hi, rhs_hi, start=first, stop=False)
                nc.tensor.matmul(dst, lhs_hi, rhs_lo, start=False, stop=False)
                return nc.tensor.matmul(dst, lhs_lo, rhs_hi, start=False, stop=last)

            def transpose_x(S, b, c):
                for i in range(2):
                    for dt in range(KD):
                        ins = nc.tensor.transpose(lg_bank[c % 2][:, (2 * dt + i) * P:(2 * dt + i + 1) * P],
                                                  x_raw[:, NT - 2 * c - 2 + i, dt * P:(dt + 1) * P], ident[:, :])
                ins.then_inc(S.xT, 1)

            def scores(b, J):
                for k in range(NCH):
                    if CHUNKS[k][0] == J:
                        scores_chunk(b, k)

            def scores_chunk(b, k):
                J, c0, c1 = CHUNKS[k]
                if not (isinstance(b, int) and b == 0 and k < 2):
                    pe.wait_ge(F.leaky, NCH * b + k - 1)
                dst = lg_bank[k % 2][:, 0:(c1 - c0) * P]
                for dt in range(KD):
                    rows = slice(J * P, (J + 1) * P)
                    cols = slice(c0 * P, c1 * P)
                    ins = split_products(dst, gT_hi[:, dt, rows], gT_lo[:, dt, rows], hT_hi[:, dt, cols],
                                         hT_lo[:, dt, cols], dt == 0, dt == KD - 1)
                ins.then_inc(F.logits, 1)

            def transpose_codes(S, b, t):
                pe.wait_ge(S.adj_loaded[t % 4], 32 * b + 16 * (t // 4) + 16)
                bank_bf = tr_bank[t % 2][:, :].bitcast(BF16)
                for J in range(NT):
                    ins = nc.tensor.transpose(bank_bf[:, J * P:(J + 1) * P],
                                              code_nat[:, t % 4, J * P:(J + 1) * P], ident_bf[:, :])
                ins.then_inc(S.codes, 1)

            def mirror(b, t):
                for m, (tt, j0, j1) in enumerate(MIRRORS):
                    if tt != t:
                        continue
                    if m >= 2:
                        pe.wait_ge(F.mirror_used, NM * b + m - 1)
                    else:
                        pe.wait_ge(F.codes_kept, NT * b + NT - 1 + m)
                    pe.wait_ge(F.tanh, NT * b + t + 1)
                    for j in range(j0, j1):
                        ins = nc.tensor.transpose(tr_bank[m % 2][:, (j - j0) * P:(j - j0 + 1) * P],
                                                  score_at(t, j, j + 1), ident[:, :])
                    ins.then_inc(F.mirror, 1)

            def aggregate0(S, b, t, prev):
                pe.wait_ge(S.lo0, NT * b + t + 1)
                if t == 0:
                    pe.wait_ge(S.h_lo, 4 * b + 4)
                if t >= 2:
                    pe.wait_ge(S.resid0, NT * b + t - 1)
                elif prev:
                    pe.wait_ge(S.relu, NT * b + t - 1)
                for J in range(NT):
                    ins = split_products(acc_bank[t % 2][:, 0:D], coef_hi[:, t % 4, J, :], coef_lo[:, t % 4, J, :],
                                         h_hi[:, J, :], h_lo[:, J, :], J == 0, J == NT - 1)
                ins.then_inc(S.agg0, 1)

            def transpose_x1(S, b, t):
                pe.wait_ge(S.x1, NT * b + t + 1)
                for dt in range(KD):
                    ins = nc.tensor.transpose(xt_bank[:, dt * P:(dt + 1) * P], x1[:, t, dt * P:(dt + 1) * P],
                                              ident[:, :])
                ins.then_inc(S.x1T, 1)

            def spread_s(S, b, t):
                pe.wait_ge(S.sd, NT * b + t + 1)
                return nc.tensor.transpose(spread_bank, sd[:, t, 1:2].broadcast_to([P, P]), ident[:, :])

            def project(S, b, t, prev):
                pe.wait_ge(S.x1T_lo, NT * b + t + 1)
                if t >= 1 or prev:
                    pe.wait_ge(S.H_lo, NT * b + t)
                if t >= 1:
                    spread_s(S, b, t - 1)
                elif prev:
                    pe.wait_ge(S.G, NT * b)
                for dt in range(KD):
                    ins = split_products(hh_bank[:, 0:HC], x1T_hi[:, t % 2, dt, :], x1T_lo[:, t % 2, dt, :],
                                         W_hi[:, dt, :], W_lo[:, dt, :], dt == 0, dt == KD - 1)
                ins.then_inc(S.proj, 1)

            def spread_last(S, b):
                pe.wait_ge(S.H_lo, NT * b + NT)
                spread_s(S, b, NT - 1).then_inc(S.spread, 1)

            def aggregate1(S, b, t):
                pe.wait_ge(S.lo1, NT * b + t + 1)
                if t == 0:
                    pe.wait_ge(S.ones_lo, b + 1)
                    pe.wait_ge(S.H_lo, NT * b + NT)
                if t >= 2:
                    pe.wait_ge(S.relu, NT * b + t - 1)
                else:
                    pe.wait_ge(S.resid0, NT * b + t + 7)
                for J in range(NT):
                    ins = split_products(acc_bank[t % 2][:, 0:HC], coef_hi[:, t % 4, J, :],
                                         coef_lo[:, t % 4, J, :], H_hi[:, J, :], H_lo[:, J, :],
                                         J == 0, J == NT - 1)
                ins.then_inc(S.agg1, 1)

            def graph(b, prev, nxt):
                for t in range(NT):
                    if t >= 3:
                        pe.wait_ge(F.x1T_lo, NT * b + t - 2)
                        transpose_x1(F, b, t - 2)
                    if 1 <= t and t + 3 < NT:
                        mirror(b, t + 3)
                    if nxt and t == 0:
                        pe.wait_ge(F.x_loaded, 16 * (b + 2))
                        pe.wait_ge(F.leaky, NCH * (b + 1))
                        transpose_x(F, b + 1, 0)
                    aggregate0(F, b, t, prev)
                    if t == 2:
                        if prev:
                            pe.wait_ge(F.x1T_lo, NT * b)
                        transpose_x1(F, b, 0)
                    if nxt and t in (1, 3, 4):
                        c = {1: 1, 3: 2, 4: 3}[t]
                        if c >= 2:
                            pe.wait_ge(F.xT_lo, 4 * (b + 1) + c - 1)
                        transpose_x(F, b + 1, c)
                    if nxt and 5 <= t < 7:
                        if t == 5:
                            pe.wait_ge(F.xT_lo, 4 * (b + 1) + 3)
                        else:
                            pe.wait_ge(F.xT_lo, 4 * (b + 1) + 4)
                        scores_chunk(b + 1, t - 5)
                    if t >= 2:
                        project(F, b, t - 2, prev)
                pe.wait_ge(F.x1T_lo, NT * b + 6)
                transpose_x1(F, b, 6)
                if nxt:
                    scores_chunk(b + 1, 2)
                project(F, b, 6, prev)
                if nxt:
                    scores_chunk(b + 1, 3)
                pe.wait_ge(F.x1T_lo, NT * b + 7)
                transpose_x1(F, b, 7)
                if nxt:
                    scores_chunk(b + 1, 4)
                project(F, b, 7, prev)
                if nxt:
                    scores_chunk(b + 1, 5)
                    for t in range(2):
                        pe.wait_ge(F.mirror_used, NM * b + NM - 1 + t)
                        transpose_codes(F, b + 1, t)
                spread_last(F, b)
                if nxt:
                    scores_chunk(b + 1, 6)
                    scores_chunk(b + 1, 7)
                    pe.wait_ge(F.codes_kept, NT * (b + 1) + 1)
                    transpose_codes(F, b + 1, 2)
                for t in range(NT):
                    if nxt and t + 3 > NT:
                        mirror(b + 1, t + 3 - NT)
                    aggregate1(F, b, t)
                    if nxt and t + 3 == NT:
                        mirror(b + 1, 0)
                    if nxt and t + 3 < NT:
                        pe.wait_ge(F.codes_kept, NT * (b + 1) + t + 2)
                        transpose_codes(F, b + 1, t + 3)
                    if nxt and t == 0:
                        scores_chunk(b + 1, 8)
                    if nxt and 1 <= t < 3:
                        scores(b + 1, 2 + t)
                if nxt:
                    mirror(b + 1, 3)

            pe.wait_ge(ident_made, 4)
            pe.wait_ge(F.x_loaded, 16)
            for c in range(4):
                if c >= 2:
                    pe.wait_ge(F.xT_lo, c - 1)
                transpose_x(F, 0, c)
            pe.wait_ge(F.xT_lo, 4)
            for J in ROWS:
                scores(0, J)
            for t in range(NT):
                if t >= 2:
                    pe.wait_ge(F.codes_kept, t - 1)
                transpose_codes(F, 0, t)
            for t in range(4):
                mirror(0, t)
            pe.wait_ge(weights_ready, 1)
            graph(0, False, True)
            with pe.Fori(1, LAST) as b:
                graph(b, True, True)
            graph(LAST, True, False)

            pe.wait_ge(flag_step, 5)
            pe.wait_ge(consts_made, 4)
            nc.tensor.matmul(xt_bank[0:1, 0:1], flag_f[:, :], ones_col[:, :], start=True,
                             stop=True).then_inc(flag_summed, 1)

            pe.wait_ge(flag_ready, 1)
            flag = pe.value_load(flag_i[0:1, 0:1], min_val=0, max_val=512)
            with pe.If(flag > 0):
                with pe.Fori(0, B) as b:
                    pe.wait_ge(GEN.x_loaded, 16 * b + 16)
                    for c in range(4):
                        if c >= 2:
                            pe.wait_ge(GEN.xT_lo, 4 * b + c - 1)
                        transpose_x(GEN, b, c)
                    pe.wait_ge(GEN.xT_lo, 4 * b + 4)
                    for t in range(NT):
                        if t >= 2:
                            pe.wait_ge(GEN.codes_kept, NT * b + t - 1)
                        transpose_codes(GEN, b, t)
                        for k in range(KINDS):
                            n = KINDS * (NT * b + t) + k
                            pe.wait_ge(GEN.g_lo, n + 1)
                            for J in range(NT):
                                dst = lg_bank[J // 4][:, (J % 4) * P:(J % 4 + 1) * P]
                                rows = slice(J * P, (J + 1) * P)
                                for dt in range(KD):
                                    ins = split_products(dst, hT_hi[:, dt, rows], hT_lo[:, dt, rows],
                                                         gT_hi[:, dt, 0:P], gT_lo[:, dt, 0:P],
                                                         dt == 0, dt == KD - 1)
                            ins.then_inc(GEN.logits, 1)
                        aggregate0(GEN, b, t, False)
                        if t:
                            pe.wait_ge(GEN.x1T_lo, NT * b + t)
                        transpose_x1(GEN, b, t)
                        project(GEN, b, t, False)
                    spread_last(GEN, b)
                    for t in range(NT):
                        aggregate1(GEN, b, t)
                    pe.wait_ge(GEN.out_stored[0], 16 * NT * (b + 1))


_INS = ["x", "adj", "L0_gnn_a0", "L0_gnn_a1", "L0_gnn_a2", "L0_gnn_a3", "L0_gnn_bias", "L1_gnn_W", "L1_gnn_a"]


def kernel(**inputs):
    import concourse.bacc as bacc
    from concourse.bass_utils import run_bass_kernel_spmd

    nc = bacc.Bacc("TRN2", target_bir_lowering=False, num_devices=1)
    arrays, args = {}, []
    for name in _INS:
        v = np.ascontiguousarray(inputs[name])
        arrays["in_" + name] = v
        args.append(nc.dram_tensor("in_" + name, v.shape, mybir.dt.from_np(v.dtype), kind="ExternalInput").ap())
    shape = inputs["x"].shape
    out = nc.dram_tensor("out_0", shape, FP32, kind="ExternalOutput").ap()
    two_graph_layers(nc, *args, out)
    r = run_bass_kernel_spmd(nc, [arrays], core_ids=[0])
    return r.results[0]["out_0"]
```
